# Optimizing a Trainium2 kernel written in Bass

```python
import numpy as np
import jax
import jax.numpy as jnp

def _softmax(x, axis=-1):
    return jax.nn.softmax(x, axis=axis)

def _gelu(x):
    return jax.nn.gelu(x, approximate=True)

def _silu(x):
    return jax.nn.silu(x)

def _sigmoid(x):
    return jax.nn.sigmoid(x)

def _layernorm(x, axis=-1, eps=1e-05):
    m = jnp.mean(x, axis=axis, keepdims=True)
    v = jnp.var(x, axis=axis, keepdims=True)
    return (x - m) / jnp.sqrt(v + eps)

def _scatter_add(tgt, idx, src, axis=0):
    return tgt.at[idx].add(src)

def _segment_sum(src, seg, n):
    return jax.ops.segment_sum(src, seg, n)
kernel_name = 'mk_seq_postln_d1_jaxref_r8_17afe9'

def setup_inputs(seed: int=0):
    np.random.seed(seed)
    _w = jnp.asarray

    def _L0_attn_setup():
        import jax, jax.numpy as jnp
        import numpy as np
        DIM = 128
        H = 16
        HD = DIM // H
        R = 8
        QK = 32
        B = 4
        S = 128
        EPS = 1e-05

        def _lin(x, W, b):
            return x @ W.T + b

        def _ln(x, g, b):
            m = x.mean(-1, keepdims=True)
            v = ((x - m) ** 2).mean(-1, keepdims=True)
            return (x - m) / jnp.sqrt(v + EPS) * g + b
        key = jax.random.key(seed)
        ks = iter(jax.random.split(key, 32))

        def w(shape, fan):
            s = 1.0 / np.sqrt(fan)
            return jax.random.uniform(next(ks), shape, jnp.float32, -s, s)
        d = {}
        d['x'] = jax.random.normal(next(ks), (B, S, DIM), jnp.float32)
        d['Wq'] = w((DIM, DIM), DIM)
        d['bq'] = w((DIM,), DIM)
        d['Wk'] = w((DIM, DIM), DIM)
        d['bk'] = w((DIM,), DIM)
        d['Wv'] = w((HD * R, DIM), DIM)
        d['bv'] = w((HD * R,), DIM)
        d['Wqv'] = w((QK * H, DIM), DIM)
        d['bqv'] = w((QK * H,), DIM)
        d['Ws'] = w((1, HD + QK), HD + QK)
        d['bs'] = w((1,), HD + QK)
        d['Wf'] = w((DIM, DIM), DIM)
        d['bf'] = w((DIM,), DIM)
        d['Wr1'] = w((2 * DIM, DIM), DIM)
        d['br1'] = w((2 * DIM,), DIM)
        d['Wr2'] = w((DIM, 2 * DIM), 2 * DIM)
        d['br2'] = w((DIM,), 2 * DIM)
        d['g1'] = jnp.ones((DIM,), jnp.float32)
        d['b1'] = jnp.zeros((DIM,), jnp.float32)
        d['g2'] = jnp.ones((DIM,), jnp.float32)
        d['b2'] = jnp.zeros((DIM,), jnp.float32)
        return d
    _L0_attn_in = _L0_attn_setup()

    def _L0_ffn_setup():
        import jax, jax.numpy as jnp
        import numpy as np
        DIM = 128
        DEPTH = 2
        HEADS = 8
        DIM_HEAD = 64
        WINDOW = 64
        INNER = HEADS * DIM_HEAD
        HID = int(DIM * 4 * 2 / 3)
        B, N = (2, 1024)
        QK_SCALE = 8.0

        def shift_token(t):
            t1, t2 = jnp.split(t, 2, axis=-1)
            t2 = jnp.pad(t2, ((0, 0), (1, 0), (0, 0)))[:, :-1]
            return jnp.concatenate([t1, t2], axis=-1)

        def l2norm(t):
            return t / jnp.clip(jnp.linalg.norm(t, axis=-1, keepdims=True), 1e-12)

        def rotate_half(x):
            x1, x2 = jnp.split(x, 2, axis=-1)
            return jnp.concatenate([-x2, x1], axis=-1)

        def rotary_xpos(q, k):
            n = q.shape[-2]
            half_idx = jnp.arange(0, DIM_HEAD, 2, dtype=jnp.float32)
            inv_freq = 1.0 / 10000.0 ** (half_idx / DIM_HEAD)
            t = jnp.arange(n, dtype=jnp.float32)
            freqs = t[:, None] * inv_freq[None, :]
            freqs = jnp.concatenate([freqs, freqs], axis=-1)
            base = (half_idx + 0.4 * DIM_HEAD) / (1.4 * DIM_HEAD)
            power = (t - n // 2) / float(WINDOW // 2)
            scale = base[None, :] ** power[:, None]
            scale = jnp.concatenate([scale, scale], axis=-1)
            cos, sin = (jnp.cos(freqs), jnp.sin(freqs))
            q = q * cos * scale + rotate_half(q) * sin * scale
            k = k * cos / scale + rotate_half(k) * sin / scale
            return (q, k)

        def local_attention(q, k, v):
            b, h, n, d = q.shape
            w = n // WINDOW
            bq = q.reshape(b, h, w, WINDOW, d) * QK_SCALE
            bk = k.reshape(b, h, w, WINDOW, d)
            bv = v.reshape(b, h, w, WINDOW, d)

            def look_around(t):
                p = jnp.pad(t, ((0, 0), (0, 0), (1, 0), (0, 0), (0, 0)))
                return jnp.concatenate([p[:, :, :w], p[:, :, 1:]], axis=3)
            bk, bv = (look_around(bk), look_around(bv))
            bt = jnp.arange(n).reshape(w, WINDOW)
            btp = jnp.pad(bt, ((1, 0), (0, 0)), constant_values=-1)
            btk = jnp.concatenate([btp[:w], btp[1:]], axis=1)
            sim = jnp.einsum('bhwid,bhwjd->bhwij', bq, bk)
            i = bt[:, :, None]
            j = btk[:, None, :]
            mask = (i < j) | (i > j + WINDOW) | (j == -1)
            sim = jnp.where(mask, -jnp.finfo(sim.dtype).max, sim)
            attn = jax.nn.softmax(sim, axis=-1)
            out = jnp.einsum('bhwij,bhwjd->bhwid', attn, bv)
            return out.reshape(b, h, n, d)

        def _layer(x, wqkv, qs, ksc, wo, lg, lb, w1, b1, w2, b2):
            b, n, _ = x.shape
            h = shift_token(x)
            qkv = h @ wqkv
            q, k, v = jnp.split(qkv, 3, axis=-1)
            to_heads = lambda t: t.reshape(b, n, HEADS, DIM_HEAD).transpose(0, 2, 1, 3)
            q, k, v = (to_heads(q), to_heads(k), to_heads(v))
            q = l2norm(q) * qs
            k = l2norm(k) * ksc
            q, k = rotary_xpos(q, k)
            o = local_attention(q, k, v)
            o = o.transpose(0, 2, 1, 3).reshape(b, n, INNER)
            x = x + o @ wo
            h = shift_token(x)
            mu = h.mean(-1, keepdims=True)
            var = h.var(-1, keepdims=True)
            h = (h - mu) / jnp.sqrt(var + 1e-05) * lg + lb
            h = h @ w1 + b1
            a, g = jnp.split(h, 2, axis=-1)
            h = a * jax.nn.gelu(g, approximate=False)
            x = x + h @ w2 + b2
            return x
        key = jax.random.key(seed)
        ks = jax.random.split(key, 6)
        return {'x': jax.random.normal(ks[0], (B, N, DIM), jnp.float32), 'wqkv': jax.random.normal(ks[1], (DEPTH, DIM, 3 * INNER), jnp.float32) * 0.02, 'q_scale': jnp.ones((DEPTH, DIM_HEAD), jnp.float32), 'k_scale': jnp.ones((DEPTH, DIM_HEAD), jnp.float32), 'wo': jax.random.normal(ks[2], (DEPTH, INNER, DIM), jnp.float32) * 0.02, 'ln_g': jnp.ones((DEPTH, DIM), jnp.float32), 'ln_b': jnp.zeros((DEPTH, DIM), jnp.float32), 'w1': jax.random.normal(ks[3], (DEPTH, DIM, 2 * HID), jnp.float32) * 0.02, 'b1': jnp.zeros((DEPTH, 2 * HID), jnp.float32), 'w2': jax.random.normal(ks[4], (DEPTH, HID, DIM), jnp.float32) * 0.02, 'b2': jnp.zeros((DEPTH, DIM), jnp.float32)}
    _L0_ffn_in = _L0_ffn_setup()
    _d = {'L0_attn_x': _L0_attn_in['x'], 'L0_attn_Wq': _L0_attn_in['Wq'], 'L0_attn_bq': _L0_attn_in['bq'], 'L0_attn_Wk': _L0_attn_in['Wk'], 'L0_attn_bk': _L0_attn_in['bk'], 'L0_attn_Wv': _L0_attn_in['Wv'], 'L0_attn_bv': _L0_attn_in['bv'], 'L0_attn_Wqv': _L0_attn_in['Wqv'], 'L0_attn_bqv': _L0_attn_in['bqv'], 'L0_attn_Ws': _L0_attn_in['Ws'], 'L0_attn_bs': _L0_attn_in['bs'], 'L0_attn_Wf': _L0_attn_in['Wf'], 'L0_attn_bf': _L0_attn_in['bf'], 'L0_attn_Wr1': _L0_attn_in['Wr1'], 'L0_attn_br1': _L0_attn_in['br1'], 'L0_attn_Wr2': _L0_attn_in['Wr2'], 'L0_attn_br2': _L0_attn_in['br2'], 'L0_attn_g1': _L0_attn_in['g1'], 'L0_attn_b1': _L0_attn_in['b1'], 'L0_attn_g2': _L0_attn_in['g2'], 'L0_attn_b2': _L0_attn_in['b2'], 'L0_ffn_wqkv': _L0_ffn_in['wqkv'], 'L0_ffn_q_scale': _L0_ffn_in['q_scale'], 'L0_ffn_k_scale': _L0_ffn_in['k_scale'], 'L0_ffn_wo': _L0_ffn_in['wo'], 'L0_ffn_ln_g': _L0_ffn_in['ln_g'], 'L0_ffn_ln_b': _L0_ffn_in['ln_b'], 'L0_ffn_w1': _L0_ffn_in['w1'], 'L0_ffn_b1': _L0_ffn_in['b1'], 'L0_ffn_w2': _L0_ffn_in['w2'], 'L0_ffn_b2': _L0_ffn_in['b2']}
    _x0 = _d['L0_attn_x']
    _d['L0_attn_x'] = jax.random.normal(jax.random.fold_in(jax.random.key(seed), 1), (8, 512, 128), dtype=_x0.dtype)
    del _x0
    return _d

def reference(L0_attn_x, L0_attn_Wq, L0_attn_bq, L0_attn_Wk, L0_attn_bk, L0_attn_Wv, L0_attn_bv, L0_attn_Wqv, L0_attn_bqv, L0_attn_Ws, L0_attn_bs, L0_attn_Wf, L0_attn_bf, L0_attn_Wr1, L0_attn_br1, L0_attn_Wr2, L0_attn_br2, L0_attn_g1, L0_attn_b1, L0_attn_g2, L0_attn_b2, L0_ffn_wqkv, L0_ffn_q_scale, L0_ffn_k_scale, L0_ffn_wo, L0_ffn_ln_g, L0_ffn_ln_b, L0_ffn_w1, L0_ffn_b1, L0_ffn_w2, L0_ffn_b2):

    def _L0_attn_ref(x, Wq, bq, Wk, bk, Wv, bv, Wqv, bqv, Ws, bs, Wf, bf, Wr1, br1, Wr2, br2, g1, b1, g2, b2):
        import jax, jax.numpy as jnp
        import numpy as np
        DIM = 128
        H = 16
        HD = DIM // H
        R = 8
        QK = 32
        B = 4
        S = 128
        EPS = 1e-05

        def _lin(x, W, b):
            return x @ W.T + b

        def _ln(x, g, b):
            m = x.mean(-1, keepdims=True)
            v = ((x - m) ** 2).mean(-1, keepdims=True)
            return (x - m) / jnp.sqrt(v + EPS) * g + b
        b, n, _ = x.shape
        res = x
        xn = _ln(x, g1, b1)
        q = _lin(xn, Wq, bq).reshape(b, n, H, HD) / np.sqrt(HD).astype(np.float32)
        k = _lin(xn, Wk, bk).reshape(b, n, H, HD)
        score = jax.nn.softmax(jnp.einsum('bihd,bjhd->bhij', q, k), axis=-1)
        v = _lin(xn, Wv, bv).reshape(b, n, R, HD)
        out = jnp.einsum('bhij,bjrd->bihrd', score, v)
        qv = _lin(xn, Wqv, bqv).reshape(b, n, H, 1, QK) / np.sqrt(QK).astype(np.float32)
        qv = jnp.broadcast_to(qv, (b, n, H, R, QK))
        comp = jnp.concatenate([qv, out], axis=-1) @ Ws.T + bs
        comp = jax.nn.softmax(comp, axis=3)
        out = (comp * out).sum(axis=3).reshape(b, n, DIM)
        out = res + _lin(out, Wf, bf)
        res2 = out
        on = _ln(out, g2, b2)
        ffn = _lin(jax.nn.relu(_lin(on, Wr1, br1)), Wr2, br2)
        return res2 + ffn

    def _L0_ffn_ref(x, wqkv, q_scale, k_scale, wo, ln_g, ln_b, w1, b1, w2, b2):
        import jax, jax.numpy as jnp
        import numpy as np
        DIM = 128
        DEPTH = 2
        HEADS = 8
        DIM_HEAD = 64
        WINDOW = 64
        INNER = HEADS * DIM_HEAD
        HID = int(DIM * 4 * 2 / 3)
        B, N = (2, 1024)
        QK_SCALE = 8.0

        def shift_token(t):
            t1, t2 = jnp.split(t, 2, axis=-1)
            t2 = jnp.pad(t2, ((0, 0), (1, 0), (0, 0)))[:, :-1]
            return jnp.concatenate([t1, t2], axis=-1)

        def l2norm(t):
            return t / jnp.clip(jnp.linalg.norm(t, axis=-1, keepdims=True), 1e-12)

        def rotate_half(x):
            x1, x2 = jnp.split(x, 2, axis=-1)
            return jnp.concatenate([-x2, x1], axis=-1)

        def rotary_xpos(q, k):
            n = q.shape[-2]
            half_idx = jnp.arange(0, DIM_HEAD, 2, dtype=jnp.float32)
            inv_freq = 1.0 / 10000.0 ** (half_idx / DIM_HEAD)
            t = jnp.arange(n, dtype=jnp.float32)
            freqs = t[:, None] * inv_freq[None, :]
            freqs = jnp.concatenate([freqs, freqs], axis=-1)
            base = (half_idx + 0.4 * DIM_HEAD) / (1.4 * DIM_HEAD)
            power = (t - n // 2) / float(WINDOW // 2)
            scale = base[None, :] ** power[:, None]
            scale = jnp.concatenate([scale, scale], axis=-1)
            cos, sin = (jnp.cos(freqs), jnp.sin(freqs))
            q = q * cos * scale + rotate_half(q) * sin * scale
            k = k * cos / scale + rotate_half(k) * sin / scale
            return (q, k)

        def local_attention(q, k, v):
            b, h, n, d = q.shape
            w = n // WINDOW
            bq = q.reshape(b, h, w, WINDOW, d) * QK_SCALE
            bk = k.reshape(b, h, w, WINDOW, d)
            bv = v.reshape(b, h, w, WINDOW, d)

            def look_around(t):
                p = jnp.pad(t, ((0, 0), (0, 0), (1, 0), (0, 0), (0, 0)))
                return jnp.concatenate([p[:, :, :w], p[:, :, 1:]], axis=3)
            bk, bv = (look_around(bk), look_around(bv))
            bt = jnp.arange(n).reshape(w, WINDOW)
            btp = jnp.pad(bt, ((1, 0), (0, 0)), constant_values=-1)
            btk = jnp.concatenate([btp[:w], btp[1:]], axis=1)
            sim = jnp.einsum('bhwid,bhwjd->bhwij', bq, bk)
            i = bt[:, :, None]
            j = btk[:, None, :]
            mask = (i < j) | (i > j + WINDOW) | (j == -1)
            sim = jnp.where(mask, -jnp.finfo(sim.dtype).max, sim)
            attn = jax.nn.softmax(sim, axis=-1)
            out = jnp.einsum('bhwij,bhwjd->bhwid', attn, bv)
            return out.reshape(b, h, n, d)

        def _layer(x, wqkv, qs, ksc, wo, lg, lb, w1, b1, w2, b2):
            b, n, _ = x.shape
            h = shift_token(x)
            qkv = h @ wqkv
            q, k, v = jnp.split(qkv, 3, axis=-1)
            to_heads = lambda t: t.reshape(b, n, HEADS, DIM_HEAD).transpose(0, 2, 1, 3)
            q, k, v = (to_heads(q), to_heads(k), to_heads(v))
            q = l2norm(q) * qs
            k = l2norm(k) * ksc
            q, k = rotary_xpos(q, k)
            o = local_attention(q, k, v)
            o = o.transpose(0, 2, 1, 3).reshape(b, n, INNER)
            x = x + o @ wo
            h = shift_token(x)
            mu = h.mean(-1, keepdims=True)
            var = h.var(-1, keepdims=True)
            h = (h - mu) / jnp.sqrt(var + 1e-05) * lg + lb
            h = h @ w1 + b1
            a, g = jnp.split(h, 2, axis=-1)
            h = a * jax.nn.gelu(g, approximate=False)
            x = x + h @ w2 + b2
            return x
        for l in range(DEPTH):
            x = _layer(x, wqkv[l], q_scale[l], k_scale[l], wo[l], ln_g[l], ln_b[l], w1[l], b1[l], w2[l], b2[l])
        return x
    x = L0_attn_x
    x = _layernorm(x + _L0_attn_ref(x, L0_attn_Wq, L0_attn_bq, L0_attn_Wk, L0_attn_bk, L0_attn_Wv, L0_attn_bv, L0_attn_Wqv, L0_attn_bqv, L0_attn_Ws, L0_attn_bs, L0_attn_Wf, L0_attn_bf, L0_attn_Wr1, L0_attn_br1, L0_attn_Wr2, L0_attn_br2, L0_attn_g1, L0_attn_b1, L0_attn_g2, L0_attn_b2), axis=-1)
    x = _layernorm(x + _L0_ffn_ref(x, L0_ffn_wqkv, L0_ffn_q_scale, L0_ffn_k_scale, L0_ffn_wo, L0_ffn_ln_g, L0_ffn_ln_b, L0_ffn_w1, L0_ffn_b1, L0_ffn_w2, L0_ffn_b2), axis=-1)
    return x

_drawn_inputs = setup_inputs


def setup_inputs(seed=0):
    import zlib

    import numpy as np

    out = dict(_drawn_inputs(seed))
    spreads = {'L0_attn_g1': (1.0, 0.6),
     'L0_attn_b1': (0.0, 0.8),
     'L0_attn_g2': (1.0, 0.6),
     'L0_attn_b2': (0.0, 2.0),
     'L0_ffn_q_scale': (1.0, 0.6),
     'L0_ffn_k_scale': (1.0, 0.6),
     'L0_ffn_ln_g': (1.0, 0.6),
     'L0_ffn_ln_b': (0.0, 0.8),
     'L0_ffn_b1': (0.0, 0.8),
     'L0_ffn_b2': (0.0, 0.529)}
    factors = {'L0_attn_Wq': 8.0,
     'L0_attn_bq': 8.0,
     'L0_attn_Wk': 8.0,
     'L0_attn_bk': 64.0,
     'L0_attn_Wv': 8.0,
     'L0_attn_bv': 8.0,
     'L0_attn_Wqv': 64.0,
     'L0_attn_bqv': 64.0,
     'L0_attn_Ws': 8.0,
     'L0_attn_Wf': 5.898,
     'L0_attn_br1': 45.328,
     'L0_attn_br2': 22.441,
     'L0_ffn_wqkv': 3.509,
     'L0_ffn_wo': 3.598,
     'L0_ffn_w1': 6.205,
     'L0_ffn_w2': 6.107,
     'L0_attn_bf': 8.0,
     'L0_attn_Wr1': 3.179}
    for name, (base, spread) in spreads.items():
        noise = np.random.default_rng([zlib.crc32(name.encode()), seed]).standard_normal(out[name].shape)
        drawn = base * np.exp(spread * noise) if base else spread * noise
        out[name] = jnp.asarray(drawn.astype(out[name].dtype))
    for name, factor in factors.items():
        out[name] = (out[name] * factor).astype(out[name].dtype)
    return out
```

```python
from contextlib import ExitStack

import numpy as np

import concourse.bass as bass
from concourse import mybir

F32 = mybir.dt.float32
BF16 = mybir.dt.bfloat16
ALU = mybir.AluOpType
ACT = mybir.ActivationFunctionType
AX = mybir.AxisListType.X

P = 128
B, S, D = 8, 512, 128
T = S // P
EPS = 1e-5

H, HD = 16, 8
R = 8
QK = 32
RV = R * HD
QUADS = H // 4
VC = 96
SPLIT = 3
NPROD = SPLIT * SPLIT * HD
GUARD = 96

LAYERS = 2
NH, DH = 8, 64
INNER = NH * DH
WIN = 64
PAIRS = NH // 2
HID = 341
HCH = [(0, 128), (128, 128), (256, HID - 256)]
MASKED = -3.0e38


class Event:

    def __init__(self, sem, step=1):
        self.sem, self.step, self.n = sem, step, 0


class Tick:

    def __init__(self, event, n):
        self.event, self.n = event, n


class Queue:

    def __init__(self):
        self.items = []

    def do(self, make, event=None):
        self.items.append((make, event))
        if event is None:
            return None
        event.n += event.step
        return Tick(event, event.n)

    def wait(self, *ticks):
        for t in ticks:
            if t is not None:
                self.items.append((None, t))

    def then(self, make, event):
        t = self.do(make, event)
        self.wait(t)
        return t

    def play(self, eng, turn):
        for make, x in self.items:
            if make is None:
                eng.wait_ge(x.event.sem, x.n)
            else:
                ins = make(eng, turn)
                if x is not None:
                    ins.then_inc(x.sem, x.step)


def build(nc, t, out):
    ctx = ExitStack()
    with ctx:
        def sb(name, shape, dt=F32):
            return ctx.enter_context(nc.sbuf_tensor(name, shape, dt))

        def event(name, step=1):
            ev = Event(ctx.enter_context(nc.semaphore(name)), step)
            events.append(ev)
            return ev

        events = []
        bank = [ctx.enter_context(nc.psum_tensor(f"bank{i}", [P, 512], F32)) for i in range(8)]
        free = [None] * 8

        ident = sb("ident", [P, P])
        identb = sb("identb", [P, P], BF16)
        negm_half = sb("neg_half", [P, 64])
        wq = sb("wq", [P, D]); wk = sb("wk", [P, D]); wv_all = sb("wv_all", [P, VC])
        wf = sb("wf", [P, D]); wr1 = sb("wr1", [P, 2 * D]); wr2 = sb("wr2", [P, 2, D])
        bias_v = sb("bias_v", [P, VC]); bias_f = sb("bias_f", [P, D]); bias_r2 = sb("bias_r2", [P, D])
        cols = sb("cols", [P, 32])
        ws = sb("ws", [P, HD + QK]); bs = sb("bs", [P, 1])
        wqkv = [sb(f"wqkv{l}", [P, 3 * INNER]) for l in range(LAYERS)]
        wo = [sb(f"wo{l}", [P, PAIRS, D]) for l in range(LAYERS)]
        w1 = [sb(f"w1_{l}", [P, 2 * HID]) for l in range(LAYERS)]
        w2 = [sb(f"w2_{l}", [P, 3, D]) for l in range(LAYERS)]
        bias_2 = [sb(f"bias_2_{l}", [P, D]) for l in range(LAYERS)]
        rot = [sb(f"rot{l}", [P, 4, T, DH]) for l in range(LAYERS)]
        mask = sb("mask", [P, 3, 512], BF16)
        x_in = sb("x_in", [P, T, D])
        x_a = sb("x_a", [P, T, D]); x_b = sb("x_b", [P, T, D]); x_mid = sb("x_mid", [P, T, D])
        x_out = sb("x_out", [P, T, D])
        normed = sb("normed", [P, T, D])
        stats = sb("stats", [P, T, 6]); moments = sb("moments", [P, T, 2]); rstd = sb("rstd", [P, T])
        feat = sb("feat", [P, S])
        q32 = sb("q32", [P, S]); k32 = sb("k32", [P, S])
        parts = {"q": sb("q_parts", [P, SPLIT, S], BF16), "k": sb("k_parts", [P, SPLIT, S], BF16)}
        rest = sb("rest", [P, S])
        stack = {"q": sb("q_stack", [P, H, S], BF16), "k": sb("k_stack", [P, H, S], BF16)}
        v_tok = sb("v_tok", [P, T, VC])
        pick_q = sb("pick_q", [P, T, H])
        rowmax = sb("rowmax", [P, 2, 16])
        negmax = sb("negmax", [16, 2, 2, P], BF16)
        probs = sb("probs", [P, 5, T, S])
        raw = sb("raw", [P, 4, S])
        small = sb("small", [P, S])
        rden = sb("rden", [P, T, 4]); logit = sb("logit", [P, T, 4, R]); lmax = sb("lmax", [P, T, 4])
        lexp = sb("lexp", [P, T, 4, R]); lsum = sb("lsum", [P, T, 4]); lrec = sb("lrec", [P, T, 4])
        weight = sb("weight", [P, T, 4, R])
        prod = sb("prod", [P, T, 2, R, HD])
        att = sb("att", [P, T, D])
        hid = sb("hid", [P, 3, S])
        flat = probs[:, :, :, :].rearrange("p a t s -> p (a t s)")
        at = [0]

        def over(*shape):
            n = int(np.prod(shape))
            v = flat[:, at[0]:at[0] + n]
            at[0] += n
            assert at[0] <= 5 * T * S
            names = "abcd"[:len(shape)]
            return v.rearrange(f"p ({' '.join(names)}) -> p {' '.join(names)}",
                               **{c: s for c, s in zip(names, shape)}) if len(shape) > 1 else v

        k_all = over(PAIRS, WIN + S)
        v_odd = over(T, INNER)
        o_all = over(PAIRS, S)
        v_even = sb("v_even", [P, T + 1, INNER])
        q_diag = sb("q_diag", [P, 2, PAIRS, 2, P])
        qn = over(2, INNER); sq = over(2, INNER); t1 = over(INNER)
        q_rot = sb("q_rot", [P, 2, INNER])
        ss = sb("ss", [P, 2, NH]); rn = sb("rn", [P, 2, NH])
        wmax = sb("wmax", [P, 2, PAIRS]); wsum = sb("wsum", [P, 2, PAIRS]); wrec = sb("wrec", [P, 2, PAIRS])
        pw = sb("pw", [P, 2, PAIRS, P]); pt = sb("pt", [P, 2, PAIRS, P])
        gate = sb("gate", [P, 3, S])

        qscr = nc.dram_tensor("parts_scratch", [2, SPLIT, P, S], BF16, kind="Internal").ap()

        pe, act, dve, pool, sp = Queue(), Queue(), Queue(), Queue(), Queue()
        e_const = event("e_const", 16)
        e_load = event("e_setup_load", 16)
        s_dve = event("e_setup_dve")
        s_pool = event("e_setup_pool")

        def load(q, dst, src, ev=e_load):
            return q.do(lambda e, i: e.dma_start(dst, src), ev)

        wqv_tmp = prod[:, :, :, :, :].rearrange("p t h r d -> p (t h r d)")
        bqv_tmp = q32[:, :]
        sv = raw[:, 0, :]
        rot_src = raw[:, 1, :].rearrange("p (c t d) -> p c t d", c=2, t=4)[:, :, :, :]
        tab = probs[:, 4, 0:2, :].rearrange("p a (b t d) -> p (a b) t d", t=T, d=DH)
        scl = probs[:, 4, 2, 0:8 * DH].rearrange("p (l c d) -> p l c d", l=LAYERS, c=4)

        loads = [
            (ident, t["ident"]), (identb, t["identb"]), (mask[:, :, :], t["mask"]),
            (wq, t["WqT"]), (wk, t["WkT"]), (wv_all[:, 0:RV], t["WvT"]), (wqv_tmp, t["WqvT"]),
            (wf, t["WfT"]), (wr1, t["Wr1T"]), (wr2[:, :, :], t["Wr2T"]),
            (bias_v[:, 0:RV], t["bv"].partition_broadcast(P)), (bqv_tmp, t["bqv"].partition_broadcast(P)),
            (bias_f, t["bf"].partition_broadcast(P)), (bias_r2, t["br2"].partition_broadcast(P)),
            (cols[:, 0:1], t["bq"]), (cols[:, 1:2], t["bk"]), (cols[:, 2:3], t["g1"]), (cols[:, 3:4], t["b1"]),
            (cols[:, 4:5], t["g2"]), (cols[:, 5:6], t["b2"]), (cols[:, 6:8], t["br1"]),
            (ws, t["Ws"].partition_broadcast(P)), (bs, t["bs"].partition_broadcast(P)),
        ]
        for l in range(LAYERS):
            loads += [
                (wqkv[l], t["wqkv"][l]), (wo[l][:, :, :], t["wo"][l].rearrange("(c p) n -> p c n", p=P)),
                (w1[l], t["w1"][l]), (w2[l][:, 0:2, :], t["w2"][l, 0:256].rearrange("(c p) n -> p c n", p=P)),
                (w2[l][0:HCH[2][1], 2, :], t["w2"][l, 256:HID]),
                (bias_2[l], t["fb2"][l].partition_broadcast(P)),
                (cols[:, 8 + 8 * l:9 + 8 * l], t["ln_g"][l]), (cols[:, 9 + 8 * l:10 + 8 * l], t["ln_b"][l]),
            ]
            for half in range(2):
                for c, (o, n) in enumerate(HCH):
                    loads.append((cols[0:n, 10 + 8 * l + 3 * half + c:11 + 8 * l + 3 * half + c],
                                  t["fb1"][l, half * HID + o:half * HID + o + n]))
        loads += [(tab[:, c, :, :], t["tables"][c]) for c in range(4)]
        for l in range(LAYERS):
            for which, name in enumerate(("q_scale", "k_scale")):
                loads.append((scl[:, l, 2 * which, :], t[name][l].partition_broadcast(P)))
                for a in range(2):
                    loads.append((scl[:, l, 2 * which + 1, 32 * a:32 * a + 32],
                                  t[name][l, 32 * (1 - a):32 * (2 - a)].partition_broadcast(P)))
        for dst, src in loads:
            load(sp, dst if not hasattr(dst, "name") else dst[:, :], src)
        loaded = Tick(e_load, e_load.n)
        init = [
            (dve, stack["q"][:, :, :], 0.0), (dve, stack["k"][:, :, :], 0.0),
            (pool, v_even[:, :, :], 0.0), (pool, q_diag[:, :, :, :, :], 0.0),
            (pool, negm_half[:, :], -0.5), (pool, wv_all[:, RV:VC], 0.0), (pool, bias_v[:, RV:VC], 0.0),
        ]
        for q, dst, val in init:
            q.then(lambda e, i, dst=dst, val=val: e.memset(dst, val), s_dve if q is dve else s_pool)
        dve.then(lambda e, i: e.memset(stack["k"][GUARD:GUARD + 2, :, :], 1.0), s_dve)
        padded = Tick(s_pool, s_pool.n)
        dve.wait(loaded, padded)

        def fold(src, n, width, part, dst):
            view = src.rearrange("p (g w) -> p g w", w=width)
            tmp = sv[:, 0:n * width].rearrange("p (g w) -> p g w", w=width)
            coef = ws[:, part:part + width].unsqueeze(1).broadcast_to([P, n, width])
            dve.then(lambda e, i: e.tensor_tensor(tmp, view, coef, ALU.mult), s_dve)
            dve.then(lambda e, i: e.tensor_reduce(dst, tmp, AX, ALU.add), s_dve)

        o = RV + R
        fold(wv_all[:, 0:RV], R, HD, QK, wv_all[:, RV:o])
        fold(bias_v[:, 0:RV], R, HD, QK, bias_v[:, RV:o])
        fold(wqv_tmp, H, QK, 0, wv_all[:, o:o + H])
        fold(bqv_tmp, H, QK, 0, bias_v[:, o:o + H])
        for w in (wv_all, bias_v):
            dve.then(lambda e, i, w=w: e.tensor_scalar(w[:, o:o + H], w[:, o:o + H], float(QK) ** -0.5, None,
                                                       ALU.mult), s_dve)
        dve.then(lambda e, i: e.tensor_scalar(bias_v[:, o:o + H], bias_v[:, o:o + H], bs[:, 0:1], None, ALU.add),
                 s_dve)
        for l in range(LAYERS):
            for c in range(4):
                dve.then(lambda e, i, c=c, l=l: e.tensor_tensor(
                    rot[l][:, c, :, :], tab[:, c, :, :], scl[:, l, c, :].unsqueeze(1).broadcast_to([P, T, DH]),
                    ALU.mult), s_dve)
        ready = [Tick(s_dve, s_dve.n), Tick(s_pool, s_pool.n), Tick(e_load, e_load.n)]
        for q in (pe, act, dve, pool, sp):
            q.wait(*ready)
        setup_events = list(events)
        setup = dict(tensor=pe, scalar=act, vector=dve, gpsimd=pool, sync=sp)

        pe, act, dve, pool, sp = Queue(), Queue(), Queue(), Queue(), Queue()
        last_read = {}
        e_x = event("e_x", 16)
        e_pe = {}

        def ev(name, step=1):
            if name not in e_pe:
                e_pe[name] = event(name, step)
            return e_pe[name]

        def take(b):
            if free[b]:
                pe.wait(*free[b])

        def mm(b_out, lhsT, rhs, start, stop, event=None):
            return pe.do(lambda e, i: e.matmul(b_out, lhsT, rhs, start=start, stop=stop,
                                               skip_group_check=True), event)

        def transpose(dst, src, n, event=None):
            return pe.do(lambda e, i: e.transpose(dst, src, ident[0:n, 0:n]), event)

        def A(q, dst, src, fn, event, **kw):
            return q.do(lambda e, i: e.activation(dst, src, fn, **kw), event)

        def tt(q, dst, a, b, op, event=None):
            return q.do(lambda e, i: e.tensor_tensor(dst, a, b, op), event)

        def norm(src, dst, tag, src_ready):
            st, mo, rs = ev(f"{tag}_stats"), ev(f"{tag}_moments"), ev(f"{tag}_rstd")
            dve.wait(src_ready)
            ts = [dve.do(lambda e, i, j=j: e.bn_stats(stats[:, j, :], src[:, j, :]), st) for j in range(T)]
            dve.wait(ts[-1])
            ts = [dve.do(lambda e, i, j=j: e.bn_aggr(moments[:, j, :], stats[:, j, :]), mo) for j in range(T)]
            pool.wait(ts[-1])
            a = pool.then(lambda e, i: e.tensor_scalar(rstd[:, :], moments[:, :, 1], EPS, None, ALU.add), rs)
            a = pool.then(lambda e, i: e.tensor_tensor(rstd[:, :], rstd[:, :], negm_half[:, 0:T], ALU.pow), rs)
            dve.wait(a, ts[-1])
            done = ev(f"{tag}_normed")
            for j in range(T):
                last = dve.do(lambda e, i, j=j: e.tensor_scalar(
                    dst[:, j, :], src[:, j, :], moments[:, j, 0:1], rstd[:, j:j + 1],
                    ALU.subtract, ALU.mult), done)
            return last

        def to_feat(b, src, tag, src_ready):
            pe.wait(src_ready)
            take(b)
            e = ev(f"{tag}_turned")
            for j in range(T):
                last = transpose(bank[b][:, j * P:(j + 1) * P], src[:, j, :], P, e if j == T - 1 else None)
            return last

        sp_x = sp.do(lambda e, i: e.dma_start(x_in[:, :, :], t["x"][i].rearrange("(t p) d -> p t d", p=P)), e_x)

        n1 = norm(x_in, normed, "ln1", sp_x)
        tf = to_feat(0, normed, "ln1", n1)
        act.wait(tf)
        xf = A(act, feat[:, :], bank[0][:, :], ACT.Identity, ev("ln1_affine"),
               scale=cols[:, 2:3], bias=cols[:, 3:4])
        free[0] = [xf]

        pe.wait(xf)
        take(1)
        m = mm(bank[1][:, :], wq[:, :], feat[:, :], True, True, ev("qk_proj"))
        dve.wait(m)
        s = float(HD) ** -0.5
        qd = dve.do(lambda e, i: e.tensor_scalar(q32[:, :], bank[1][:, :], cols[:, 0:1], s, ALU.add, ALU.mult),
                    ev("q_scaled"))
        free[1] = [qd]
        take(2)
        m = mm(bank[2][:, :], wk[:, :], feat[:, :], True, True, ev("qk_proj"))
        dve.wait(m)
        kd = dve.do(lambda e, i: e.tensor_scalar(k32[:, :], bank[2][:, :], cols[:, 1:2], None, ALU.add),
                    ev("k_biased"))
        free[2] = [kd]
        take(3)
        for j in range(T):
            m = mm(bank[3][:, j * VC:(j + 1) * VC], feat[:, j * P:(j + 1) * P], wv_all[:, :], True, True,
                   ev("v_proj") if j == T - 1 else None)
        dve.wait(m)
        bv = dve.do(lambda e, i: e.tensor_tensor(
            v_tok[:, :, :], bank[3][:, 0:T * VC].rearrange("p (t c) -> p t c", t=T),
            bias_v[:, :].unsqueeze(1).broadcast_to([P, T, VC]), ALU.add), ev("v_biased"))
        free[3] = [bv]
        pool.wait(bv)
        pool.then(lambda e, i: e.tensor_copy(pick_q[:, :, :], v_tok[:, :, RV + R:RV + R + H]), ev("v_ones"))
        pool.then(lambda e, i: e.memset(v_tok[:, :, RV + R:VC], 0.0), ev("v_ones"))
        v_done = pool.then(lambda e, i: e.memset(v_tok[:, :, RV + R:RV + R + 1], 1.0), ev("v_ones"))

        for src, ready_, name, idx in ((q32, qd, "q", 0), (k32, kd, "k", 1)):
            e = ev(f"{name}_split")
            pr = parts[name]
            dve.wait(ready_)
            dve.then(lambda e_, i, pr=pr, src=src: e_.tensor_copy(pr[:, 0, :], src[:, :]), e)
            dve.then(lambda e_, i, pr=pr, src=src: e_.tensor_tensor(rest[:, :], src[:, :], pr[:, 0, :],
                                                                    ALU.subtract), e)
            dve.then(lambda e_, i, pr=pr: e_.tensor_copy(pr[:, 1, :], rest[:, :]), e)
            last = dve.then(lambda e_, i, pr=pr: e_.tensor_tensor(pr[:, 2, :], rest[:, :], pr[:, 1, :],
                                                                  ALU.subtract), e)
            sp.wait(last)
            w = sp.do(lambda e_, i, pr=pr, idx=idx: e_.dma_start(
                qscr[idx].rearrange("a p n -> p a n"), pr[:, :, :]), ev(f"{name}_to_scratch", 16))
            sp.wait(w)
            for a in range(SPLIT):
                for c in range(SPLIT):
                    row = (a * SPLIT + c) * HD
                    part = a if name == "q" else c
                    last = sp.do(lambda e_, i, row=row, part=part, idx=idx, name=name: e_.dma_start(
                        stack[name][row:row + HD, :, :],
                        qscr[idx, part].rearrange("(h d) n -> d h n", d=HD)), ev(f"{name}_stacked", 16))
            if name == "q":
                q_st = last
            else:
                k_st = last

        qs, ks = stack["q"], stack["k"]
        S_BANKS, T_BANKS, RAW, SMALL, TOK, MISC = (0, 1), (2, 3), 4, 5, 6, 7
        pe.wait(q_st, k_st)
        e_s, e_m = ev("scores"), ev("row_max")
        e_t, e_p = ev("scores_t"), ev("probs")
        max_tick, guard_tick, prob_tick = {}, {}, {}
        pv_tick, small_tick = {}, {}
        counter = [0, 0]

        def scores(h):
            g, hh = divmod(h, 4)
            if hh == 0 and g >= 2:
                dve.wait(guard_tick[g - 2, "read"])
            for j in range(T):
                b = S_BANKS[counter[0] % 2]
                counter[0] += 1
                take(b)
                m = mm(bank[b][:, :], qs[0:GUARD, h, j * P:(j + 1) * P], ks[0:GUARD, h, :], True, True, e_s)
                dve.wait(m)
                c = hh * T + j
                r = dve.do(lambda e, i, b=b, c=c, g=g: e.tensor_reduce(rowmax[:, g % 2, c:c + 1], bank[b][:, :],
                                                                      AX, ALU.max), e_m)
                free[b] = [r]
            max_tick[h] = r

        def guard(g):
            pe.wait(max_tick[4 * g + 3])
            take(MISC)
            m = transpose(bank[MISC][0:16, 0:P], rowmax[:, g % 2, :], P, ev("max_turned"))
            dve.wait(m)
            guard_tick[g, "read"] = m
            if g >= 2:
                dve.wait(guard_tick[g - 2, "sent"])
            dve.then(lambda e, i, g=g: e.tensor_scalar(negmax[:, g % 2, 0, :], bank[MISC][0:16, 0:P], -1.0, None,
                                                       ALU.mult), ev("guard_split"))
            r = dve.do(lambda e, i, g=g: e.scalar_tensor_tensor(
                out=negmax[:, g % 2, 1, :], in0=bank[MISC][0:16, 0:P], scalar=-1.0,
                in1=negmax[:, g % 2, 0, :], op0=ALU.mult, op1=ALU.subtract), ev("guard_split"))
            free[MISC] = [r]
            sp.wait(r)
            for a in range(2):
                d = sp.do(lambda e, i, g=g, a=a: e.dma_start(
                    qs[GUARD + a:GUARD + a + 1, 4 * g:4 * g + 4, :].rearrange("p h n -> p (h n)"),
                    negmax[:, g % 2, a, :]), ev(f"guard_rows{g}", 16))
            guard_tick[g, "sent"] = d

        def scores_t(h):
            g = h // 4
            if h % 4 == 0:
                pe.wait(guard_tick[g, "sent"])
            slot = h % 5
            for j in range(T):
                b = T_BANKS[counter[1] % 2]
                counter[1] += 1
                take(b)
                m = mm(bank[b][:, :], ks[0:GUARD + 2, h, j * P:(j + 1) * P], qs[0:GUARD + 2, h, :],
                       True, True, e_t)
                act.wait(m)
                if j == 0 and h >= 5:
                    act.wait(small_tick[(h - 5) // 4])
                if j == 0 and h == 0 and over_read:
                    act.wait(*over_read)
                r = A(act, probs[:, slot, j, :], bank[b][:, :], ACT.Exp, e_p)
                free[b] = [r]
            prob_tick[h] = r

        raw_tick = {}

        def values(h0):
            pe.wait(prob_tick[h0 + 1], v_done)
            take(RAW)
            for j in range(T):
                for hh in range(2):
                    m = mm(bank[RAW][64 * hh:64 * hh + 64, :], v_tok[:, j, 0:RV], probs[:, (h0 + hh) % 5, j, :],
                           j == 0, j == T - 1, ev("raw_values") if j == T - 1 and hh == 1 else None)
            pair = h0 // 2
            act.wait(m)
            if pair >= 4:
                act.wait(raw_tick[pair - 4, "read"])
            r = A(act, raw[:, pair % 4, :], bank[RAW][:, :], ACT.Copy, ev("raw_out"))
            free[RAW] = [r]
            raw_tick[pair, "out"] = r

        w_tick = {}

        def weights(g):
            take(SMALL)
            for j in range(T):
                for hh in range(4):
                    m = mm(bank[SMALL][32 * hh:32 * hh + 32, :], v_tok[:, j, RV:VC],
                           probs[:, (4 * g + hh) % 5, j, :], j == 0, j == T - 1,
                           ev("small_values") if j == T - 1 and hh == 3 else None)
            small_tick[g] = m
            act.wait(m)
            if g:
                act.wait(w_tick[g - 1, "turned"])
            r = A(act, small[:, :], bank[SMALL][:, :], ACT.Copy, ev("small_out"))
            free[SMALL] = [r]
            pe.wait(r)
            take(TOK)
            for j in range(T):
                m = transpose(bank[TOK][:, j * P:(j + 1) * P], small[:, j * P:(j + 1) * P], P,
                              ev("small_turned") if j == T - 1 else None)
            w_tick[g, "turned"] = m
            tok = bank[TOK][:, :].rearrange("p (t g c) -> p t g c", t=T, g=4)
            e = ev("pick")
            wide = lambda a: a[:, :, :].unsqueeze(3).broadcast_to([P, T, 4, R])
            dve.wait(m)
            if g:
                dve.wait(w_tick[g - 1, "used"])
            dve.then(lambda e_, i: e_.reciprocal(rden[:, :, :], tok[:, :, :, R]), e)
            r = dve.then(lambda e_, i: e_.tensor_tensor(logit[:, :, :, :], tok[:, :, :, 0:R], wide(rden),
                                                        ALU.mult), e)
            free[TOK] = [r]
            pq = pick_q[:, :, 4 * g:4 * g + 4].unsqueeze(3).broadcast_to([P, T, 4, R])
            dve.then(lambda e_, i: e_.tensor_tensor(logit[:, :, :, :], logit[:, :, :, :], pq, ALU.add), e)
            dve.then(lambda e_, i: e_.tensor_reduce(lmax[:, :, :], logit[:, :, :, :], AX, ALU.max), e)
            r = dve.do(lambda e_, i: e_.tensor_tensor(logit[:, :, :, :], logit[:, :, :, :], wide(lmax),
                                                      ALU.subtract), e)
            act.wait(r)
            r = A(act, lexp[:, :, :, :], logit[:, :, :, :], ACT.Exp, ev("pick_exp"))
            dve.wait(r)
            dve.then(lambda e_, i: e_.tensor_reduce(lsum[:, :, :], lexp[:, :, :, :], AX, ALU.add), e)
            dve.then(lambda e_, i: e_.reciprocal(lrec[:, :, :], lsum[:, :, :]), e)
            dve.then(lambda e_, i: e_.tensor_tensor(lrec[:, :, :], lrec[:, :, :], rden[:, :, :], ALU.mult), e)
            w_tick[g, "w"] = dve.then(lambda e_, i: e_.tensor_tensor(weight[:, :, :, :], lexp[:, :, :, :],
                                                                     wide(lrec), ALU.mult), e)

        def combine(pair):
            g, half = divmod(pair, 2)
            pe.wait(raw_tick[pair, "out"])
            take(TOK)
            for j in range(T):
                m = transpose(bank[TOK][:, j * P:(j + 1) * P], raw[:, pair % 4, j * P:(j + 1) * P], P,
                              ev("raw_turned") if j == T - 1 else None)
            raw_tick[pair, "read"] = m
            dve.wait(m)
            if pair:
                dve.wait(w_tick["prod"])
            wv = weight[:, :, 2 * half:2 * half + 2, :].rearrange("p t h r -> p t (h r)")
            wv = wv.unsqueeze(3).broadcast_to([P, T, 2 * R, HD])
            r = dve.then(lambda e, i: e.tensor_tensor(
                prod[:, :, :, :, :].rearrange("p t h r d -> p t (h r) d"),
                bank[TOK][:, :].rearrange("p (t x d) -> p t x d", t=T, d=HD), wv, ALU.mult), ev("weighted"))
            free[TOK] = [r]
            if half:
                w_tick[g, "used"] = r
            w_tick["prod"] = w_tick["att"] = dve.do(lambda e, i: e.tensor_reduce(
                att[:, :, 16 * pair:16 * pair + 16].rearrange("p t (h d) -> p t h d", d=HD),
                prod[:, :, :, :, :].rearrange("p t h r d -> p t h d r"), AX, ALU.add), ev("combined"))

        over_read = []
        pe_over = len(act.items)
        for h in range(4):
            scores(h)
        guard(0)
        for g in range(QUADS):
            for hh in range(4):
                if g + 1 < QUADS:
                    scores(4 * (g + 1) + hh)
                scores_t(4 * g + hh)
                if hh == 2:
                    values(4 * g)
            if g + 1 < QUADS:
                guard(g + 1)
            values(4 * g + 2)
            weights(g)
            combine(2 * g)
            combine(2 * g + 1)

        tf = to_feat(0, att, "att", w_tick["att"])
        act.wait(tf)
        r = A(act, feat[:, :], bank[0][:, :], ACT.Copy, ev("att_feat"))
        free[0] = [r]
        pe.wait(r)
        take(1)
        for j in range(T):
            m = mm(bank[1][:, j * P:(j + 1) * P], feat[:, j * P:(j + 1) * P], wf[:, :], True, True,
                   ev("wf") if j == T - 1 else None)
        b1v = bank[1][:, :].rearrange("p (t d) -> p t d", t=T)
        row = lambda a: a[:, :].unsqueeze(1).broadcast_to([P, T, D])
        e = ev("res2")
        dve.wait(m)
        r = dve.then(lambda e_, i: e_.tensor_tensor(x_a[:, :, :], b1v, x_in[:, :, :], ALU.add), e)
        free[1] = [r]
        res2 = dve.then(lambda e_, i: e_.tensor_tensor(x_a[:, :, :], x_a[:, :, :], row(bias_f), ALU.add), e)
        n2 = norm(x_a, normed, "ln2", res2)
        tf = to_feat(0, normed, "ln2", n2)
        act.wait(tf)
        r = A(act, feat[:, :], bank[0][:, :], ACT.Identity, ev("ln2_affine"), scale=cols[:, 4:5], bias=cols[:, 5:6])
        free[0] = [r]
        dve.wait(n2)
        both = dve.then(lambda e_, i: e_.tensor_tensor(x_a[:, :, :], x_a[:, :, :], x_in[:, :, :], ALU.add), e)
        x_read = both
        both = dve.then(lambda e_, i: e_.tensor_tensor(x_a[:, :, :], x_a[:, :, :], row(bias_r2), ALU.add), e)
        pe.wait(r)
        for c in range(2):
            take(2 + c)
            m = mm(bank[2 + c][:, :], wr1[:, c * P:(c + 1) * P], feat[:, :], True, True, ev("mlp1"))
            act.wait(m)
            r = A(act, hid[:, c, :], bank[2 + c][:, :], ACT.Relu, ev("relu"), bias=cols[:, 6 + c:7 + c])
            free[2 + c] = [r]
        pe.wait(r)
        take(1)
        for j in range(T):
            for c in range(2):
                m = mm(bank[1][:, j * P:(j + 1) * P], hid[:, c, j * P:(j + 1) * P], wr2[:, c, :], c == 0, c == 1,
                       ev("mlp2") if j == T - 1 and c == 1 else None)
        dve.wait(m)
        r = dve.then(lambda e_, i: e_.tensor_tensor(x_a[:, :, :], x_a[:, :, :], b1v, ALU.add), e)
        free[1] = [r]
        x_done = norm(x_a, x_b, "ln3", r)

        QB, KB, VB, TB, W_BANKS, PTB, OB = 0, 1, 2, 3, (4, 5), 6, 7
        half2 = lambda v: v.rearrange("p (h a d) -> p h a d", a=2, d=DH // 2)
        wt = {}
        zero_pad = ev("k_pad")
        dve.wait(x_done)
        kz = dve.do(lambda e_, i: e_.memset(k_all[:, :, 0:WIN], 0.0), zero_pad)

        def layer(l, x_done):
            L = f"l{l}_"
            x_l, x_n = (x_b, x_mid) if l == 0 else (x_mid, x_out)
            c0 = 8 + 8 * l

            def shifted(b, tag, ready_):
                act.wait(ready_)
                z = act.do(lambda e_, i: e_.memzero(feat[64:P, 0:1]), ev(tag))
                A(act, feat[0:64, :], bank[b][0:64, :], ACT.Copy, ev(tag))
                r = A(act, feat[64:P, 1:S], bank[b][64:P, 0:S - 1], ACT.Copy, ev(tag))
                free[b] = [r]
                return r

            tf = to_feat(0, x_l, L + "x", x_done)
            hf = shifted(0, L + "shift", tf)

            def project(j):
                pe.wait(hf)
                for b in (QB, KB, VB):
                    take(b)
                    m = mm(bank[b][:, :], feat[:, j * P:(j + 1) * P], wqkv[l][:, b * INNER:(b + 1) * INNER],
                           True, True, ev("qkv"))
                    wt[b] = m
                act.wait(wt[QB])
                if "ss" in wt:
                    act.wait(wt["ss"])
                A(act, sq[:, 0, :], bank[QB][:, :], ACT.Square, ev("squares"))
                act.wait(wt[KB])
                s_ = A(act, sq[:, 1, :], bank[KB][:, :], ACT.Square, ev("squares"))
                act.wait(wt[VB])
                if ("v", j) in wt:
                    act.wait(wt["v", j], wt["ve", j])
                vo = A(act, v_odd[:, j, :], bank[VB][:, :], ACT.Copy, ev("v_odd"))
                free[VB] = [vo]
                pool.wait(vo)
                if ("pve", j) in wt:
                    pool.wait(wt["pve", j])
                if ("pve", j + 1) in wt:
                    pool.wait(wt["pve", j + 1])
                pool.then(lambda e_, i, j=j: e_.tensor_copy(v_even[0:64, j, :], v_odd[0:64, j, :]), ev("v_even"))
                wt["ve", j] = pool.then(lambda e_, i, j=j: e_.tensor_copy(v_even[64:P, j + 1, :],
                                                                        v_odd[64:P, j, :]), ev("v_even"))
                dve.wait(s_)
                if "rn" in wt:
                    dve.wait(wt["rn"])
                wt["ss"] = dve.do(lambda e_, i: e_.tensor_reduce(
                    ss[:, :, :], sq[:, :, :].rearrange("p a (h d) -> p a h d", d=DH), AX, ALU.add), ev("sumsq"))
                pool.wait(wt["ss"])
                if "qn" in wt:
                    pool.wait(wt["qn"])
                fs = ss[:, :, :].rearrange("p a h -> p (a h)")
                fr = rn[:, :, :].rearrange("p a h -> p (a h)")
                pool.then(lambda e_, i: e_.tensor_scalar(fr, fs, 1e-24, None, ALU.max), ev("rnorm"))
                r = wt["rn"] = pool.then(lambda e_, i: e_.tensor_tensor(fr, fr, negm_half[:, 0:2 * NH], ALU.pow),
                                       ev("rnorm"))
                dve.wait(r)
                for a, b in ((0, QB), (1, KB)):
                    e_ = ev("rotate")
                    if ("qnr", a) in wt:
                        dve.wait(wt["qnr", a])
                    n_ = dve.then(lambda e2, i, a=a, b=b: e2.tensor_tensor(
                        qn[:, a, :].rearrange("p (h d) -> p h d", d=DH),
                        bank[b][:, :].rearrange("p (h d) -> p h d", d=DH),
                        rn[:, a, :].unsqueeze(2).broadcast_to([P, NH, DH]), ALU.mult), e_)
                    free[b] = [n_]
                    wt["qn"] = n_
                    pool.wait(n_)
                    if ("qt", a) in wt:
                        pool.wait(wt["qt", a])
                    r1 = pool.then(lambda e2, i, a=a, j=j: e2.tensor_tensor(
                        q_rot[:, a, :].rearrange("p (h d) -> p h d", d=DH),
                        qn[:, a, :].rearrange("p (h d) -> p h d", d=DH),
                        rot[l][:, 2 * a, j, :].unsqueeze(1).broadcast_to([P, NH, DH]), ALU.mult), ev("rot_cos"))
                    v, w = half2(qn[:, a, :]), half2(t1[:, :])
                    for u in range(2):
                        sn = rot[l][:, 2 * a + 1, j, 32 * u:32 * u + 32].unsqueeze(1).broadcast_to([P, NH, 32])
                        r2 = dve.do(lambda e2, i, u=u, v=v, w=w, sn=sn: e2.tensor_tensor(
                            w[:, :, u, :], v[:, :, 1 - u, :], sn, ALU.mult), e_)
                    wt["qnr", a] = r1
                    dve.wait(r1, r2)
                    wt["rot", a] = dve.then(lambda e2, i, a=a: e2.tensor_tensor(
                        q_rot[:, a, :], q_rot[:, a, :], t1[:, :], ALU.add), e_)

            def turn(j):
                for a in range(2):
                    pe.wait(wt["rot", a])
                    take(TB)
                    for pr_ in range(PAIRS):
                        m = transpose(bank[TB][:, pr_ * P:(pr_ + 1) * P], q_rot[:, a, pr_ * P:(pr_ + 1) * P], P,
                                      ev("qk_turned") if pr_ == PAIRS - 1 else None)
                    wt["qt", a] = m
                    if a == 0:
                        act.wait(m)
                        if ("qd", j % 2) in wt:
                            act.wait(wt["qd", j % 2])
                        for u in range(2):
                            v = bank[TB][64 * u:64 * u + 64, :].rearrange("p (c w n) -> p c w n", c=PAIRS, w=2)
                            r = A(act, q_diag[64 * u:64 * u + 64, j % 2, :, :, 64 * u:64 * u + 64], v, ACT.Copy,
                                  ev("q_diag"))
                        wt["q ready"] = r
                    else:
                        dve.wait(m)
                        if l or j:
                            for x in ("ksr",):
                                if (x, j) in wt:
                                    dve.wait(wt[x, j])
                        r = dve.do(lambda e_, i, j=j: e_.tensor_copy(
                            k_all[:, :, WIN + j * P:WIN + (j + 1) * P],
                            bank[TB][:, :].rearrange("p (c n) -> p c n", c=PAIRS)), ev("k_feat"))
                        wt["k ready"] = r
                    free[TB] = [r]

            def window(w):
                j, odd = divmod(w, 2)
                b = W_BANKS[w % 2]
                n = w % 2
                pe.wait(wt["q ready"], wt["k ready"], kz)
                take(b)
                mk = 0 if odd else (2 if w == 0 else 1)
                mm(bank[b][:, :], identb[:, :], mask[:, mk, :], True, False)
                for c in range(PAIRS):
                    keys = k_all[:, c, w * WIN:(w + 2) * WIN]
                    for u in range(1 if odd else 2):
                        kk = keys if odd else keys[:, (1 - u) * WIN:(2 - u) * WIN]
                        oo = bank[b][:, c * P:(c + 1) * P] if odd else bank[b][:, c * P + u * WIN:c * P + (u + 1) * WIN]
                        last = bool(c == PAIRS - 1 and (odd or u == 1))
                        m = mm(oo, q_diag[:, j % 2, c, odd, :], kk, False, last, ev("w_scores") if last else None)
                wt["qd", j % 2] = m
                wt["ksr", j] = m
                if j + 1 < T:
                    wt["ksr", j] = m
                dve.wait(m)
                if ("wm", n) in wt:
                    dve.wait(wt["wm", n])
                v = bank[b][:, :].rearrange("p (c k) -> p c k", c=PAIRS)
                dve.then(lambda e_, i: e_.tensor_reduce(wmax[:, n, :], v, AX, ALU.max), ev("w_max"))
                r = dve.do(lambda e_, i: e_.tensor_scalar(wmax[:, n, :], wmax[:, n, :], -1.0, None, ALU.mult),
                           ev("w_max"))
                act.wait(r)
                if ("pw", n) in wt:
                    act.wait(wt["pw", n])
                if ("ws", n) in wt:
                    act.wait(wt["ws", n])
                for c in range(PAIRS):
                    r = A(act, pw[:, n, c, :], v[:, c, :], ACT.Exp, ev("w_exp"), bias=wmax[:, n, c:c + 1],
                          accum_out=wsum[:, n, c:c + 1])
                free[b] = [r]
                wt["wm", n] = r
                dve.wait(r)
                if ("wr", n) in wt:
                    dve.wait(wt["wr", n])
                r = wt["ws", n] = dve.do(lambda e_, i: e_.reciprocal(wrec[:, n, :], wsum[:, n, :]), ev("w_rec"))
                pool.wait(r)
                r = pool.then(lambda e_, i: e_.tensor_tensor(
                    pw[:, n, :, :], pw[:, n, :, :], wrec[:, n, :].unsqueeze(2).broadcast_to([P, PAIRS, P]),
                    ALU.mult), ev("w_norm"))
                wt["wr", n] = r
                wt["p", w] = r

            def outputs(w):
                j, odd = divmod(w, 2)
                n = w % 2
                pe.wait(wt["p", w])
                take(PTB)
                for c in range(PAIRS):
                    m = transpose(bank[PTB][:, c * P:(c + 1) * P], pw[:, n, c, :], P,
                                  ev("p_turned") if c == PAIRS - 1 else None)
                wt["pw", n] = m
                dve.wait(m)
                if ("pt", n) in wt:
                    dve.wait(wt["pt", n])
                r = dve.do(lambda e_, i: e_.tensor_copy(pt[:, n, :, :],
                                                        bank[PTB][:, :].rearrange("p (c k) -> p c k", c=PAIRS)),
                           ev("p_out"))
                free[PTB] = [r]
                pe.wait(r, wt["ve", j])
                take(OB)
                vv = v_odd if odd else v_even
                for c in range(PAIRS):
                    m = mm(bank[OB][:, c * P:(c + 1) * P], vv[:, j, c * P:(c + 1) * P], pt[:, n, c, :], True, True,
                           ev("w_out") if c == PAIRS - 1 else None)
                wt["pt", n] = m
                wt["v", j] = m
                if not odd:
                    wt["pve", j] = m
                    if j == T - 1:
                        pass
                act.wait(m)
                if ("o", j) in wt:
                    act.wait(wt["o", j])
                for u in range(2):
                    r = A(act, o_all[64 * u:64 * u + 64, :, w * WIN:(w + 1) * WIN],
                          bank[OB][64 * u:64 * u + 64, :].rearrange("p (c x n) -> p c x n", c=PAIRS, x=2)[:, :, u, :],
                          ACT.Copy, ev("o_feat"))
                free[OB] = [r]
                wt["o ready", w] = r

            project(0)
            turn(0)
            for j in range(T):
                window(2 * j)
                window(2 * j + 1)
                if j + 1 < T:
                    project(j + 1)
                outputs(2 * j)
                outputs(2 * j + 1)
                if j + 1 < T:
                    turn(j + 1)
            take(0)
            for j in range(T):
                pe.wait(wt["o ready", 2 * j + 1])
                for c in range(PAIRS):
                    m = mm(bank[0][:, j * P:(j + 1) * P], o_all[:, c, j * P:(j + 1) * P], wo[l][:, c, :],
                           c == 0, c == PAIRS - 1, ev("wo") if (c, j) == (PAIRS - 1, T - 1) else None)
                wt["o", j] = m
            for j in range(T):
                wt["o", j] = m
            e = ev(L + "res")
            dve.wait(m)
            b0v = bank[0][:, :].rearrange("p (t d) -> p t d", t=T)
            r = dve.then(lambda e_, i: e_.tensor_tensor(x_a[:, :, :], b0v, x_l[:, :, :], ALU.add), e)
            free[0] = [r]
            tf = to_feat(1, x_a, L + "y", r)
            hf2 = shifted(1, L + "shift2", tf)
            pe.wait(hf2)
            take(2)
            for j in range(T):
                m = transpose(bank[2][:, j * P:(j + 1) * P], feat[:, j * P:(j + 1) * P], P,
                              ev(L + "back") if j == T - 1 else None)
            b2v = bank[2][:, :].rearrange("p (t d) -> p t d", t=T)
            nn = norm(b2v, normed, L + "ln", m)
            free[2] = [nn]
            tf = to_feat(1, normed, L + "n", nn)
            act.wait(tf)
            r = A(act, feat[:, :], bank[1][:, :], ACT.Identity, ev(L + "affine"),
                  scale=cols[:, c0:c0 + 1], bias=cols[:, c0 + 1:c0 + 2])
            free[1] = [r]
            r2 = dve.then(lambda e_, i: e_.tensor_tensor(x_a[:, :, :], x_a[:, :, :], row(bias_2[l]), ALU.add), e)
            pe.wait(r)
            for c, (o_, n_) in enumerate(HCH):
                take(4 + c % 2)
                mg = mm(bank[4 + c % 2][0:n_, :], w1[l][:, HID + o_:HID + o_ + n_], feat[:, :], True, True,
                        ev("gate_in"))
                act.wait(mg)
                if ("gate", c) in wt:
                    act.wait(wt["gate", c])
                rg = A(act, gate[0:n_, c, :], bank[4 + c % 2][0:n_, :], ACT.Gelu, ev("gelu"),
                       bias=cols[0:n_, c0 + 5 + c:c0 + 6 + c])
                free[4 + c % 2] = [rg]
                take(6 + c % 2)
                ma = mm(bank[6 + c % 2][0:n_, :], w1[l][:, o_:o_ + n_], feat[:, :], True, True, ev("up_in"))
                dve.wait(rg, ma)
                if "hid" in wt:
                    dve.wait(wt["hid"])
                rh = wt["gate", c] = dve.do(lambda e_, i, c=c, n_=n_: e_.scalar_tensor_tensor(
                    out=hid[0:n_, c, :], in0=bank[6 + c % 2][0:n_, :], scalar=cols[0:n_, c0 + 2 + c:c0 + 3 + c],
                    in1=gate[0:n_, c, :], op0=ALU.add, op1=ALU.mult), ev("gated"))
                free[6 + c % 2] = [rh]
            pe.wait(rh)
            take(3)
            for j in range(T):
                for c, (o_, n_) in enumerate(HCH):
                    m = mm(bank[3][:, j * P:(j + 1) * P], hid[0:n_, c, j * P:(j + 1) * P], w2[l][0:n_, c, :],
                           c == 0, c == 2, ev("mlp_out") if (j, c) == (T - 1, 2) else None)
            wt["hid"] = m
            dve.wait(m)
            b3v = bank[3][:, :].rearrange("p (t d) -> p t d", t=T)
            x_done = dve.then(lambda e_, i: e_.tensor_tensor(x_n[:, :, :], x_a[:, :, :], b3v, ALU.add), e)
            free[3] = [x_done]
            return x_done

        for l in range(LAYERS):
            x_done = layer(l, x_done)

        r = dve.then(lambda e_, i: e_.tensor_tensor(x_a[:, :, :], x_b[:, :, :], x_out[:, :, :], ALU.add),
                     ev("last_res"))
        e_out = ev("stored", 16)
        r = norm(x_a, x_out, "ln4", r)
        sp.wait(r)
        st = sp.do(lambda e_, i: e_.dma_start(out[i].rearrange("(t p) d -> p t d", p=P), x_out[:, :, :]), e_out)

        loop = dict(tensor=pe, scalar=act, vector=dve, gpsimd=pool, sync=sp)

        def play(queues, turn):
            with nc.Block() as block:
                for name, decorate in dict(tensor=block.tensor, scalar=block.scalar, vector=block.vector,
                                           gpsimd=block.gpsimd, sync=block.sync).items():
                    @decorate
                    def _(eng, name=name):
                        queues[name].play(eng, turn)
                        if name == "sync":
                            for v in events:
                                if v.n and (v in setup_events) == (queues is setup):
                                    eng.wait_ge(v.sem, v.n)

        play(setup, None)
        numbers = sorted(v.sem.num for v in events if v not in setup_events)
        assert numbers == list(range(numbers[0], numbers[-1] + 1))
        with nc.Fori(0, t["x"].shape[0], 1) as i:
            play(loop, i)
            nc.sync.sem_clear(range(numbers[0], numbers[-1] + 1))
            nc.all_engine_barrier()


def kernel(**inputs):
    import ml_dtypes
    import concourse.bacc as bacc
    from concourse.bass_utils import run_bass_kernel_spmd

    v = {k.replace("L0_attn_", "").replace("L0_ffn_", "f:"): np.asarray(a) for k, a in inputs.items()}
    col = lambda a: np.ascontiguousarray(a.reshape(-1, 1))
    rowv = lambda a: np.ascontiguousarray(a.reshape(-1))
    f = np.float32
    half = np.arange(0, DH, 2).astype(f)
    inv = (f(1.0) / (f(10000.0) ** (half / f(DH)))).astype(f)
    pos = np.arange(S).astype(f)
    ang = (pos[:, None] * inv[None, :]).astype(f)
    ang = np.concatenate([ang, ang], -1)
    base = (half + f(0.4 * DH)) / f(1.4 * DH)
    power = (pos - S // 2) / f(WIN // 2)
    sc = (base[None, :] ** power[:, None]).astype(f)
    sc = np.concatenate([sc, sc], -1)
    sign = np.where(np.arange(DH) < DH // 2, f(-1), f(1))[None, :]
    cos, sin = np.cos(ang).astype(f), np.sin(ang).astype(f) * sign
    tables = np.stack([cos * sc * f(8.0), sin * sc * f(8.0), cos / sc, sin / sc]).astype(f)
    tables = np.ascontiguousarray(tables.reshape(4, T, P, DH).transpose(0, 2, 1, 3))
    i = (np.arange(P) % WIN)[:, None]
    jj = np.arange(2 * WIN)[None, :]
    bad = (jj > WIN + i) | (jj < i)
    swap = lambda m: np.concatenate([m[:, WIN:], m[:, :WIN]], 1)
    masks = [bad, swap(bad), swap(bad | (jj < WIN))]
    mask = np.stack([np.tile(np.where(m, f(MASKED), f(0)), (1, PAIRS)) for m in masks], 1)
    arrays = {
        "x": v["x"], "ident": np.eye(P, dtype=f), "identb": np.eye(P).astype(ml_dtypes.bfloat16),
        "mask": np.ascontiguousarray(mask.astype(ml_dtypes.bfloat16)), "tables": tables,
        "WqT": np.ascontiguousarray(v["Wq"].T), "WkT": np.ascontiguousarray(v["Wk"].T),
        "WvT": np.ascontiguousarray(v["Wv"].T), "WqvT": np.ascontiguousarray(v["Wqv"].T),
        "WfT": np.ascontiguousarray(v["Wf"].T), "Wr1T": np.ascontiguousarray(v["Wr1"].T),
        "Wr2T": np.ascontiguousarray(v["Wr2"].T.reshape(2, P, D).transpose(1, 0, 2)),
        "bv": rowv(v["bv"]), "bqv": rowv(v["bqv"]), "bf": rowv(v["bf"]), "br2": rowv(v["br2"]),
        "bq": col(v["bq"]), "bk": col(v["bk"]), "g1": col(v["g1"]), "b1": col(v["b1"]),
        "g2": col(v["g2"]), "b2": col(v["b2"]), "br1": np.ascontiguousarray(v["br1"].reshape(2, P).T),
        "Ws": rowv(v["Ws"]), "bs": v["bs"],
        "wqkv": v["f:wqkv"], "wo": v["f:wo"], "w1": v["f:w1"], "w2": v["f:w2"],
        "fb2": v["f:b2"].reshape(LAYERS, D), "fb1": v["f:b1"].reshape(LAYERS, 2 * HID, 1),
        "ln_g": v["f:ln_g"].reshape(LAYERS, D, 1), "ln_b": v["f:ln_b"].reshape(LAYERS, D, 1),
        "q_scale": v["f:q_scale"].reshape(LAYERS, DH), "k_scale": v["f:k_scale"].reshape(LAYERS, DH),
    }
    arrays = {"in_" + k: np.ascontiguousarray(a) for k, a in arrays.items()}
    nc = bacc.Bacc("TRN2", target_bir_lowering=False, num_devices=1)
    tensors = {k[3:]: nc.dram_tensor(k, list(a.shape), mybir.dt.from_np(a.dtype), kind="ExternalInput").ap()
               for k, a in arrays.items()}
    out = nc.dram_tensor("out_0", list(v["x"].shape), F32, kind="ExternalOutput").ap()
    build(nc, tensors, out)
    r = run_bass_kernel_spmd(nc, [arrays], core_ids=[0])
    return r.results[0]["out_0"]
```

```python
from contextlib import ExitStack

import numpy as np

import concourse.bass as bass
from concourse import mybir

F32 = mybir.dt.float32
BF16 = mybir.dt.bfloat16
ALU = mybir.AluOpType
ACT = mybir.ActivationFunctionType
AX = mybir.AxisListType.X

P = 128
B, S, D = 8, 512, 128
T = S // P
EPS = 1e-5

H, HD = 16, 8
R = 8
QK = 32
RV = R * HD
QUADS = H // 4
VC = 96
SPLIT = 3
NPROD = SPLIT * SPLIT * HD
GUARD = 96

LAYERS = 2
NH, DH = 8, 64
INNER = NH * DH
WIN = 64
PAIRS = NH // 2
HID = 341
HCH = [(0, 114), (114, 114), (228, HID - 228)]
MASKED = -3.0e38


class Event:

    def __init__(self, sem, step):
        self.sem, self.step, self.n = sem, step, 0


class Tick:

    def __init__(self, event, n, time):
        self.event, self.n, self.time = event, n, time


class Queue:

    def __init__(self, fixed, column, landing):
        self.items, self.now = [], 0.0
        self.fixed, self.column, self.landing = fixed, column, landing

    def do(self, make, event=None, columns=P):
        self.items.append((make, event))
        self.now += self.fixed + columns * self.column
        if event is None:
            return None
        event.n += event.step
        return Tick(event, event.n, self.now + self.landing)

    def wait(self, *ticks):
        for x in ticks:
            if x is not None:
                self.items.append((None, x))
                self.now = max(self.now, x.time)

    def then(self, make, event, columns=P):
        t = self.do(make, event, columns)
        self.wait(t)
        return t

    def play(self, eng, turn):
        for make, x in self.items:
            if make is None:
                eng.wait_ge(x.event.sem, x.n)
            else:
                ins = make(eng, turn)
                if x is not None:
                    ins.then_inc(x.sem, x.step)


class Slots:

    def __init__(self, n):
        self.idle = {i: () for i in range(n)}

    def take(self, n=1):
        yield lambda: len(self.idle) >= n
        since = lambda i: (max([x.time for x in self.idle[i]], default=0.0), i)
        got = sorted(self.idle, key=since)[:n]
        ticks = [x for i in got for x in self.idle.pop(i)]
        return (got[0] if n == 1 else got), ticks

    def give(self, i, *ticks):
        self.idle[i] = ticks


RANK_LOCAL, RANK_SEARCH = 0.0, 0.0


class Steps:

    def __init__(self):
        self.processes = []

    def start(self, process, rank=0):
        self.processes.append([process, next(process), rank])

    def run(self):
        while self.processes:
            best = None
            for p in self.processes:
                want = p[1]
                if callable(want):
                    if not want():
                        continue
                    key = (-1.0, p[2])
                else:
                    key = (max([want[0].now] + [x.time for x in want[1:] if x is not None]) + p[2], p[2])
                if best is None or key < best[0]:
                    best = key, p
            p = best[1]
            if not callable(p[1]):
                p[1][0].wait(*p[1][1:])
            try:
                p[1] = next(p[0])
            except StopIteration:
                self.processes.remove(p)


def build(nc, t, out):
    ctx = ExitStack()
    with ctx:
        def sb(name, shape, dt=F32):
            return ctx.enter_context(nc.sbuf_tensor(name, shape, dt))

        events = {}

        def ev(name, step=1):
            if name not in events:
                events[name] = Event(ctx.enter_context(nc.semaphore(name)), step)
            return events[name]

        bank = [ctx.enter_context(nc.psum_tensor(f"bank{i}", [P, 512], F32)) for i in range(8)]

        ident = sb("ident", [P, P])
        identb = sb("identb", [P, P], BF16)
        neg_half = sb("neg_half", [P, 2 * NH])
        later = sb("later", [P, 2, P])
        wq = sb("wq", [P, D]); wk = sb("wk", [P, D]); wv_all = sb("wv_all", [P, VC])
        wf = sb("wf", [P, D]); wr1 = sb("wr1", [P, 2 * D]); wr2 = sb("wr2", [P, 2, D])
        bias_v = sb("bias_v", [P, VC]); bias_f = sb("bias_f", [P, D]); bias_r2 = sb("bias_r2", [P, D])
        cols = sb("cols", [P, 32])
        ws = sb("ws", [P, HD + QK]); bs = sb("bs", [P, 1])
        wqkv = [sb(f"wqkv{l}", [P, 3 * INNER]) for l in range(LAYERS)]
        wo = [sb(f"wo{l}", [P, PAIRS, D]) for l in range(LAYERS)]
        w1 = [sb(f"w1_{l}", [P, 2 * HID]) for l in range(LAYERS)]
        w2 = [sb(f"w2_{l}", [P, 3, D]) for l in range(LAYERS)]
        bias_2 = [sb(f"bias_2_{l}", [P, D]) for l in range(LAYERS)]
        rot = [sb(f"rot{l}", [P, 4, T, DH]) for l in range(LAYERS)]
        mask = sb("mask", [P, 3, P], BF16)

        x_in = sb("x_in", [P, T, D])
        x_fresh = sb("x_fresh", [P, T, D])
        norm_s = dict(normed=sb("normed_s", [P, T, D]), stats=sb("stats_s", [P, T, 6]),
                      moments=sb("moments_s", [P, T, 2]), rstd=sb("rstd_s", [P, T]))
        feat_s = sb("feat_s", [P, S])
        qs = sb("q_stack", [P, H, S], BF16)
        ks = sb("k_stack", [P, H, S], BF16)
        v_tok = sb("v_tok", [P, T, VC])
        pick_q = sb("pick_q", [P, T, H])
        rowmax = sb("rowmax", [P, 2, 16])
        negmax = sb("negmax", [16, 2, 2, P], BF16)
        NPROBS = 5
        probs = sb("probs", [P, NPROBS, T, S])
        raw = sb("raw", [P, 4, S])
        qk32 = raw[:, 0:2, :]
        parts = raw[:, 2:4, :].rearrange("p a s -> p (a s)").bitcast(BF16)[:, 0:SPLIT * S].rearrange(
            "p (c s) -> p c s", c=SPLIT)
        small = sb("small", [P, S])
        rden = sb("rden", [P, T, 4]); logit = sb("logit", [P, T, 4, R]); lmax = sb("lmax", [P, T, 4])
        lexp = sb("lexp", [P, T, 4, R]); lsum = sb("lsum", [P, T, 4]); lrec = sb("lrec", [P, T, 4])
        weight = sb("weight", [P, T, 4, R])
        prod = sb("prod", [P, T, 2, R, HD])
        att = sb("att", [P, T, D])
        x_s = att
        rest = norm_s["normed"][:, :, :].rearrange("p t d -> p (t d)")
        hid_s = raw

        x_b = sb("x_b", [P, T, D])
        x_mid = sb("x_mid", [P, T, D])
        x_att = [sb(f"x_att{l}", [P, T, D]) for l in range(LAYERS)]
        feat_l = sb("feat_l", [P, P])
        qn = sb("qn", [P, 2, INNER]); sq = sb("sq", [P, 2, INNER]); q_rot = sb("q_rot", [P, 2, INNER])
        rot_sin = sq
        ss = sb("ss", [P, 2, NH]); rn = sb("rn", [P, 2, NH])
        q_diag = [sb(f"q_diag{l}", [P, PAIRS, 2, P]) for l in range(LAYERS)]
        k_ring = [sb(f"k_ring{l}", [P, PAIRS, 2 * P]) for l in range(LAYERS)]
        v_odd = [sb(f"v_odd{l}", [P, INNER]) for l in range(LAYERS)]
        v_even = [sb(f"v_even{l}", [P, 2, INNER]) for l in range(LAYERS)]
        o_feat = [sb(f"o_feat{l}", [P, PAIRS, P]) for l in range(LAYERS)]
        NWIN = 3
        wmax = sb("wmax", [P, NWIN, PAIRS]); wsum = sb("wsum", [P, NWIN, PAIRS])
        wrec = sb("wrec", [P, NWIN, PAIRS])
        pw = sb("pw", [P, NWIN, PAIRS, P]); pt = pw
        tail = [dict(stats=sb(f"tail_stats{l}", [P, 6]), moments=sb(f"tail_moments{l}", [P, 2]),
                     rstd=sb(f"tail_rstd{l}", [P, 1]), gate=sb(f"gate{l}", [P, 3, P]),
                     hid=sb(f"hid{l}", [P, 3, P]), sum=sb(f"tail_sum{l}", [P, P])) for l in range(LAYERS)]
        for buf in tail:
            buf["normed"], buf["feat"] = buf["gate"][:, 0, :], buf["hid"][:, 0, :]

        scratch = nc.dram_tensor("parts_scratch", [2, SPLIT, P, S], BF16, kind="Internal").ap()

        def queues():
            return (Queue(0.02, 0.0017, 0.1), Queue(0.1, 0.0008, 0.2), Queue(0.07, 0.00105, 0.1),
                    Queue(0.15, 0.002, 0.1), Queue(0.1, 0.003, 2.0))

        pe, act, dve, pool, sp = queues()
        s_load, s_dve, s_pool = ev("setup_load", 16), ev("setup_dve"), ev("setup_pool")
        flat = probs[:, 4, :, :].rearrange("p t s -> p (t s)")
        wqv_tmp, bqv_tmp, fold_tmp = flat[:, 0:512], flat[:, 512:1024], flat[:, 1024:1536]
        tab = probs[:, 3, 0:2, :].rearrange("p a (b t d) -> p (a b) t d", t=T, d=DH)
        scl = probs[:, 3, 2, 0:8 * DH].rearrange("p (l c d) -> p l c d", l=LAYERS, c=4)
        loads = [
            (ident[:, :], t["ident"]), (identb[:, :], t["identb"]), (mask[:, :, :], t["mask"]), (later[:, :, :], t["later"]),
            (wq[:, :], t["WqT"]), (wk[:, :], t["WkT"]), (wv_all[:, 0:RV], t["WvT"]), (wqv_tmp, t["WqvT"]),
            (wf[:, :], t["WfT"]), (wr1[:, :], t["Wr1T"]), (wr2[:, :, :], t["Wr2T"]),
            (bias_v[:, 0:RV], t["bv"].partition_broadcast(P)), (bqv_tmp, t["bqv"].partition_broadcast(P)),
            (bias_f[:, :], t["bf"].partition_broadcast(P)), (bias_r2[:, :], t["br2"].partition_broadcast(P)),
            (cols[:, 0:1], t["bq"]), (cols[:, 1:2], t["bk"]), (cols[:, 2:3], t["g1"]), (cols[:, 3:4], t["b1"]),
            (cols[:, 4:5], t["g2"]), (cols[:, 5:6], t["b2"]), (cols[:, 6:8], t["br1"]),
            (ws[:, :], t["Ws"].partition_broadcast(P)), (bs[:, :], t["bs"].partition_broadcast(P)),
        ]
        for l in range(LAYERS):
            loads += [
                (wqkv[l][:, :], t["wqkv"][l]),
                (wo[l][:, :, :], t["wo"][l].rearrange("(c p) n -> p c n", p=P)),
                (w1[l][:, :], t["w1"][l]), (bias_2[l][:, :], t["fb2"][l].partition_broadcast(P)),
                (cols[:, 8 + 8 * l:9 + 8 * l], t["ln_g"][l]), (cols[:, 9 + 8 * l:10 + 8 * l], t["ln_b"][l]),
            ]
            loads += [(w2[l][0:n, c, :], t["w2"][l, o:o + n]) for c, (o, n) in enumerate(HCH)]
            for half in range(2):
                loads += [(cols[0:n, 10 + 8 * l + 3 * half + c:11 + 8 * l + 3 * half + c],
                           t["fb1"][l, half * HID + o:half * HID + o + n]) for c, (o, n) in enumerate(HCH)]
            for which, name in enumerate(("q_scale", "k_scale")):
                loads.append((scl[:, l, 2 * which, :], t[name][l].partition_broadcast(P)))
                loads += [(scl[:, l, 2 * which + 1, 32 * a:32 * a + 32],
                           t[name][l, 32 * (1 - a):32 * (2 - a)].partition_broadcast(P)) for a in range(2)]
        loads += [(tab[:, c, :, :], t["tables"][c]) for c in range(4)]
        for n, (dst, src) in enumerate(loads):
            loaded = (sp, act)[n % 2].do(lambda e, i, dst=dst, src=src: e.dma_start(dst, src), s_load)
        for q, e, dst, val in [
            (dve, s_dve, qs[:, :, :], 0.0), (dve, s_dve, ks[:, :, :], 0.0),
            (pool, s_pool, q_diag[0][:, :, :, :], 0.0), (pool, s_pool, q_diag[1][:, :, :, :], 0.0),
            (pool, s_pool, neg_half[:, :], -0.5), (pool, s_pool, wv_all[:, RV:VC], 0.0),
            (pool, s_pool, bias_v[:, RV:VC], 0.0),
            (dve, s_dve, ks[GUARD:GUARD + 2, :, :], 1.0),
        ]:
            padded = q.then(lambda e_, i, dst=dst, val=val: e_.memset(dst, val), e)
        dve.wait(loaded, Tick(s_pool, s_pool.n, pool.now))

        def fold(src, n, width, part, dst):
            view = src.rearrange("p (g w) -> p g w", w=width)
            tmp = fold_tmp[:, 0:n * width].rearrange("p (g w) -> p g w", w=width)
            coef = ws[:, part:part + width].unsqueeze(1).broadcast_to([P, n, width])
            dve.then(lambda e, i: e.tensor_tensor(tmp, view, coef, ALU.mult), s_dve)
            dve.then(lambda e, i: e.tensor_reduce(dst, tmp, AX, ALU.add), s_dve)

        o = RV + R
        fold(wv_all[:, 0:RV], R, HD, QK, wv_all[:, RV:o])
        fold(bias_v[:, 0:RV], R, HD, QK, bias_v[:, RV:o])
        fold(wqv_tmp, H, QK, 0, wv_all[:, o:o + H])
        fold(bqv_tmp, H, QK, 0, bias_v[:, o:o + H])
        for w in (wv_all, bias_v):
            dve.then(lambda e, i, w=w: e.tensor_scalar(w[:, o:o + H], w[:, o:o + H], float(QK) ** -0.5, None,
                                                       ALU.mult), s_dve)
        dve.then(lambda e, i: e.tensor_scalar(bias_v[:, o:o + H], bias_v[:, o:o + H], bs[:, 0:1], None, ALU.add),
                 s_dve)
        for l in range(LAYERS):
            for c in range(4):
                dve.then(lambda e, i, c=c, l=l: e.tensor_tensor(
                    rot[l][:, c, :, :], tab[:, c, :, :], scl[:, l, c, :].unsqueeze(1).broadcast_to([P, T, DH]),
                    ALU.mult), s_dve)
        setup = (pe, act, dve, pool, sp)

        def section(with_search, with_local):
            for v in events.values():
                v.n = 0
            pe, act, dve, pool, sp = queues()
            steps = Steps()
            banks = Slots(8)
            done = {}

            def need(*keys):
                yield lambda: all(k in done for k in keys)
                return [done[k] for k in keys]

            def take(n=1):
                got, readers = yield from banks.take(n)
                yield pe, *readers
                return got

            def mm(b_out, lhsT, rhs, start, stop, event=None):
                n = 1
                for x in rhs.shape[1:]:
                    n *= x
                n = n // 4 if rhs.dtype == BF16 else n if lhsT.shape[1] > 64 else n // 2
                return pe.do(lambda e, i: e.matmul(b_out, lhsT, rhs, start=start, stop=stop,
                                                   skip_group_check=True), event, n)

            def transpose(dst, src, event=None):
                return pe.do(lambda e, i: e.transpose(dst, src, ident[:, :]), event, P // 4)

            def size(a):
                n = 1
                for x in a.shape[1:]:
                    n *= x
                return n

            def A(dst, src, fn, event, **kw):
                return act.do(lambda e, i: e.activation(dst, src, fn, **kw), event, size(dst))

            def TT(q, dst, a, b, op, event):
                return q.do(lambda e, i: e.tensor_tensor(dst, a, b, op), event, size(dst))

            def norm(src, dst, n, buf, tag, src_ready):
                stats, moments, rstd = buf["stats"], buf["moments"], buf["rstd"]
                yield dve, src_ready
                for j in range(n):
                    x = dve.do(lambda e, i, j=j: e.bn_stats(stats[:, j, :], src[:, j, :]), ev(f"{tag}_stats"))
                yield dve, x
                for j in range(n):
                    x = dve.do(lambda e, i, j=j: e.bn_aggr(moments[:, j, :], stats[:, j, :]),
                               ev(f"{tag}_moments"), 16)
                yield pool, x
                r = pool.do(lambda e, i: e.tensor_scalar(rstd[:, :], moments[:, :, 1], EPS, None, ALU.add),
                            ev(f"{tag}_rstd"), n)
                yield pool, r
                r = pool.do(lambda e, i: e.tensor_tensor(rstd[:, :], rstd[:, :], neg_half[:, 0:n], ALU.pow),
                            ev(f"{tag}_rstd"), n)
                yield dve, r, x
                for j in range(n):
                    last = dve.do(lambda e, i, j=j: e.tensor_scalar(
                        dst[:, j, :], src[:, j, :], moments[:, j, 0:1], rstd[:, j:j + 1],
                        ALU.subtract, ALU.mult), ev(f"{tag}_normed"))
                return last

            def to_feat(src, tag, src_ready):
                yield pe, src_ready
                b = yield from take()
                for j in range(T):
                    last = transpose(bank[b][:, j * P:(j + 1) * P], src[:, j, :],
                                     ev(f"{tag}_turned") if j == T - 1 else None)
                return b, last

            tiles = lambda b: bank[b][:, :].rearrange("p (t d) -> p t d", t=T)
            row = lambda a: a[:, :].unsqueeze(1).broadcast_to([P, T, D])

            def search(offset):
                x_ld = sp.do(lambda e, i: e.dma_start(
                    x_in[:, :, :], t["x"][i + offset if i is not None else 0].rearrange("(t p) d -> p t d", p=P)),
                    ev("x_loaded", 16))
                n1 = yield from norm(x_in, norm_s["normed"], T, norm_s, "ln1", x_ld)
                b, tf = yield from to_feat(norm_s["normed"], "ln1", n1)
                yield act, tf
                xf = A(feat_s[:, :], bank[b][:, :], ACT.Identity, ev("ln1_affine"),
                       scale=cols[:, 2:3], bias=cols[:, 3:4])
                banks.give(b, xf)
                yield pe, xf
                scaled = []
                for a, w in enumerate((wq, wk)):
                    b = yield from take()
                    m = mm(bank[b][:, :], w[:, :], feat_s[:, :], True, True, ev("qk_proj"))
                    s = float(HD) ** -0.5 if a == 0 else 1.0
                    yield dve, m
                    r = dve.do(lambda e, i, a=a, b=b, s=s: e.tensor_scalar(
                        qk32[:, a, :], bank[b][:, :], cols[:, a:a + 1], s, ALU.add, ALU.mult), ev("qk_scaled"),
                        S)
                    banks.give(b, r)
                    scaled.append(r)
                steps.start(value_projection(), RANK_SEARCH)
                sent = None
                for a, (dst, name) in enumerate(((qs, "q"), (ks, "k"))):
                    e = ev("split")
                    yield dve, scaled[a], n1, sent
                    dve.then(lambda e_, i, a=a: e_.tensor_copy(parts[:, 0, :], qk32[:, a, :]), e, S)
                    dve.then(lambda e_, i, a=a: e_.tensor_tensor(rest, qk32[:, a, :], parts[:, 0, :],
                                                                 ALU.subtract), e, S)
                    dve.then(lambda e_, i: e_.tensor_copy(parts[:, 1, :], rest), e, S)
                    last = dve.then(lambda e_, i: e_.tensor_tensor(parts[:, 2, :], rest, parts[:, 1, :],
                                                                   ALU.subtract), e, S)
                    yield sp, last
                    sent = sp.do(lambda e_, i, a=a: e_.dma_start(
                        scratch[a].rearrange("c p n -> p c n"), parts[:, :, :]), ev(f"{name}_to_scratch", 16))
                    yield sp, sent
                    for u in range(SPLIT):
                        for w in range(SPLIT):
                            r0 = (u * SPLIT + w) * HD
                            part = w if a else u
                            last = sp.do(lambda e_, i, r0=r0, part=part, a=a, dst=dst: e_.dma_start(
                                dst[r0:r0 + HD, :, :], scratch[a, part].rearrange("(h d) n -> d h n", d=HD)),
                                ev(f"{name}_stacked", 16))
                    done["stacked", a] = last
                for x in (row_maxima(), exponentials(), values(), retrieval()):
                    steps.start(x, RANK_SEARCH)
                combined, = yield from need("all combined")

                b, tf = yield from to_feat(att, "att", combined)
                yield act, tf
                r = A(feat_s[:, :], bank[b][:, :], ACT.Copy, ev("att_feat"))
                banks.give(b, r)
                yield pe, r
                b = yield from take()
                for j in range(T):
                    m = mm(bank[b][:, j * P:(j + 1) * P], feat_s[:, j * P:(j + 1) * P], wf[:, :], True, True,
                           ev("wf") if j == T - 1 else None)
                e = ev("res2")
                yield dve, m
                r = dve.do(lambda e_, i, b=b: e_.tensor_tensor(x_s[:, :, :], tiles(b), x_in[:, :, :], ALU.add),
                           e, S)
                banks.give(b, r)
                yield dve, r
                res2 = dve.do(lambda e_, i: e_.tensor_tensor(x_s[:, :, :], x_s[:, :, :], row(bias_f),
                                                             ALU.add), e, S)
                n2 = yield from norm(x_s, norm_s["normed"], T, norm_s, "ln2", res2)
                b, tf = yield from to_feat(norm_s["normed"], "ln2", n2)
                yield act, tf
                r = A(feat_s[:, :], bank[b][:, :], ACT.Identity, ev("ln2_affine"),
                      scale=cols[:, 4:5], bias=cols[:, 5:6])
                banks.give(b, r)
                e = ev("res2_pool")
                pool.wait(n2)
                pool.then(lambda e_, i: e_.tensor_tensor(x_s[:, :, :], x_s[:, :, :], x_in[:, :, :], ALU.add), e,
                          S)
                res3 = pool.then(lambda e_, i: e_.tensor_tensor(x_s[:, :, :], x_s[:, :, :], row(bias_r2),
                                                                ALU.add), e, S)
                yield pe, r
                both = yield from take(2)
                m = [mm(bank[b][:, :], wr1[:, c * P:(c + 1) * P], feat_s[:, :], True, True, ev("mlp1"))
                     for c, b in enumerate(both)]
                for c, b in enumerate(both):
                    yield act, m[c]
                    r = A(hid_s[:, c, :], bank[b][:, :], ACT.Relu, ev("relu"), bias=cols[:, 6 + c:7 + c])
                    banks.give(b, r)
                yield pe, r
                b = yield from take()
                for j in range(T):
                    for c in range(2):
                        m = mm(bank[b][:, j * P:(j + 1) * P], hid_s[:, c, j * P:(j + 1) * P], wr2[:, c, :],
                               c == 0, c == 1, ev("mlp2") if j == T - 1 and c == 1 else None)
                yield dve, m, res3
                r = dve.do(lambda e_, i, b=b: e_.tensor_tensor(x_s[:, :, :], x_s[:, :, :], tiles(b), ALU.add),
                           ev("res2"), S)
                banks.give(b, r)
                if with_local:
                    yield dve, *(yield from need("taken"))
                yield from norm(x_s, x_fresh, T, norm_s, "ln3", r)

            def value_projection():
                b = yield from take()
                for j in range(T):
                    m = mm(bank[b][:, j * VC:(j + 1) * VC], feat_s[:, j * P:(j + 1) * P], wv_all[:, :],
                           True, True, ev("v_proj") if j == T - 1 else None)
                yield dve, m
                bv = dve.do(lambda e, i: e.tensor_tensor(
                    v_tok[:, :, :], bank[b][:, 0:T * VC].rearrange("p (t c) -> p t c", t=T),
                    bias_v[:, :].unsqueeze(1).broadcast_to([P, T, VC]), ALU.add), ev("v_biased"), T * VC)
                banks.give(b, bv)
                yield pool, bv
                pool.then(lambda e, i: e.tensor_copy(pick_q[:, :, :], v_tok[:, :, RV + R:RV + R + H]),
                          ev("v_ones"))
                pool.then(lambda e, i: e.memset(v_tok[:, :, RV + R:VC], 0.0), ev("v_ones"))
                done["v"] = pool.then(lambda e, i: e.memset(v_tok[:, :, RV + R:RV + R + 1], 1.0), ev("v_ones"))

            def row_maxima():
                yield pe, done["stacked", 0], done["stacked", 1]
                for h in range(H):
                    g, hh = divmod(h, 4)
                    for j in range(T):
                        b = yield from take()
                        m = mm(bank[b][:, :], qs[0:GUARD, h, j * P:(j + 1) * P], ks[0:GUARD, h, :], True, True,
                               ev("scores"))
                        turned = None
                        if hh == 0 and j == 0 and g >= 2:
                            turned, = yield from need(("max turned", g - 2))
                        yield dve, m, turned
                        c = hh * T + j
                        r = dve.do(lambda e, i, g=g, c=c, b=b: e.tensor_reduce(
                            rowmax[:, g % 2, c:c + 1], bank[b][:, :], AX, ALU.max, negate=True), ev("row_max"),
                            S)
                        banks.give(b, r)
                    if hh == 3:
                        steps.start(guard(g, r), RANK_SEARCH)

            def guard(g, maxima):
                yield pe, maxima
                b = yield from take()
                m = transpose(bank[b][0:16, 0:P], rowmax[:, g % 2, :], ev("max_turned"))
                done["max turned", g] = m
                yield dve, m, *((yield from need(("guard sent", g - 2))) if g >= 2 else ())
                dve.then(lambda e, i: e.tensor_copy(negmax[:, g % 2, 0, :], bank[b][0:16, 0:P]),
                         ev("guard_split"))
                r = dve.do(lambda e, i: e.tensor_tensor(negmax[:, g % 2, 1, :], bank[b][0:16, 0:P],
                                                        negmax[:, g % 2, 0, :], ALU.subtract),
                           ev("guard_split"))
                banks.give(b, r)
                yield sp, r
                for a in range(2):
                    d = sp.do(lambda e, i, a=a: e.dma_start(
                        qs[GUARD + a:GUARD + a + 1, 4 * g:4 * g + 4, :].rearrange("p h n -> p (h n)"),
                        negmax[:, g % 2, a, :]), ev(f"guard_rows{g}", 16))
                done["guard sent", g] = d

            def exponentials():
                for h in range(H):
                    if h % 4 == 0:
                        yield pe, *(yield from need(("guard sent", h // 4)))
                    used = None
                    if h >= NPROBS:
                        used, = yield from need(("small", (h - NPROBS) // 4))
                    for j in range(T):
                        b = yield from take()
                        m = mm(bank[b][:, :], ks[0:GUARD + 2, h, j * P:(j + 1) * P], qs[0:GUARD + 2, h, :],
                               True, True, ev("scores_t"))
                        yield act, m, used
                        r = A(probs[:, h % NPROBS, j, :], bank[b][:, :], ACT.Exp, ev("probs"))
                        banks.give(b, r)
                        done["probs", h, j] = r

            def values():
                yield pe, *(yield from need("v"))
                for g in range(QUADS):
                    for pair in (2 * g, 2 * g + 1):
                        b = yield from take()
                        for j in range(T):
                            yield pe, *(yield from need(("probs", 2 * pair, j), ("probs", 2 * pair + 1, j)))
                            for hh in range(2):
                                m = mm(bank[b][64 * hh:64 * hh + 64, :], v_tok[:, j, 0:RV],
                                       probs[:, (2 * pair + hh) % NPROBS, j, :], j == 0, j == T - 1,
                                       ev("raw_values") if j == T - 1 and hh == 1 else None)
                        turned = None
                        if pair >= 4:
                            turned, = yield from need(("raw turned", pair - 4))
                        yield act, m, turned
                        r = A(raw[:, pair % 4, :], bank[b][:, :], ACT.Copy, ev("raw_out"))
                        banks.give(b, r)
                        done["raw", pair] = r
                    b = yield from take()
                    for j in range(T):
                        yield pe, None
                        for hh in range(4):
                            m = mm(bank[b][32 * hh:32 * hh + 32, :], v_tok[:, j, RV:VC],
                                   probs[:, (4 * g + hh) % NPROBS, j, :], j == 0, j == T - 1,
                                   ev("small_values") if j == T - 1 and hh == 3 else None)
                    done["small", g] = m
                    turned = None
                    if g:
                        turned, = yield from need(("small turned", g - 1))
                    yield act, m, turned
                    r = A(small[:, :], bank[b][:, :], ACT.Copy, ev("small_out"))
                    banks.give(b, r)
                    done["small out", g] = r

            def retrieval():
                wide = lambda a: a[:, :, :].unsqueeze(3).broadcast_to([P, T, 4, R])
                products = combined = None
                for g in range(QUADS):
                    yield pe, *(yield from need(("small out", g)))
                    b = yield from take()
                    for j in range(T):
                        m = transpose(bank[b][:, j * P:(j + 1) * P], small[:, j * P:(j + 1) * P],
                                      ev("small_turned") if j == T - 1 else None)
                    done["small turned", g] = m
                    tok = bank[b][:, :].rearrange("p (t g c) -> p t g c", t=T, g=4)
                    e = ev("pick")
                    yield dve, m
                    r = dve.do(lambda e_, i, tok=tok: e_.reciprocal(rden[:, :, :], tok[:, :, :, R]), e, 16)
                    yield dve, r
                    r = TT(dve, logit[:, :, :, :], tok[:, :, :, 0:R], wide(rden), ALU.mult, e)
                    banks.give(b, r)
                    pq = pick_q[:, :, 4 * g:4 * g + 4].unsqueeze(3).broadcast_to([P, T, 4, R])
                    yield dve, r
                    r = TT(dve, logit[:, :, :, :], logit[:, :, :, :], pq, ALU.add, e)
                    yield dve, r
                    r = dve.do(lambda e_, i: e_.tensor_reduce(lmax[:, :, :], logit[:, :, :, :], AX, ALU.max), e)
                    yield dve, r
                    r = TT(dve, logit[:, :, :, :], logit[:, :, :, :], wide(lmax), ALU.subtract, e)
                    yield act, r
                    r = A(lexp[:, :, :, :], logit[:, :, :, :], ACT.Exp, ev("pick_exp"))
                    yield dve, r
                    r = dve.do(lambda e_, i: e_.tensor_reduce(lsum[:, :, :], lexp[:, :, :, :], AX, ALU.add), e)
                    yield dve, r
                    r = dve.do(lambda e_, i: e_.reciprocal(lrec[:, :, :], lsum[:, :, :]), e, 16)
                    yield dve, r
                    r = dve.do(lambda e_, i: e_.tensor_tensor(lrec[:, :, :], lrec[:, :, :], rden[:, :, :],
                                                              ALU.mult), e, 16)
                    yield dve, r, products
                    picked = TT(dve, weight[:, :, :, :], lexp[:, :, :, :], wide(lrec), ALU.mult, e)
                    for half in range(2):
                        pair = 2 * g + half
                        yield pe, *(yield from need(("raw", pair)))
                        b = yield from take()
                        for j in range(T):
                            m = transpose(bank[b][:, j * P:(j + 1) * P], raw[:, pair % 4, j * P:(j + 1) * P],
                                          ev("raw_turned") if j == T - 1 else None)
                        done["raw turned", pair] = m
                        wv = weight[:, :, 2 * half:2 * half + 2, :].rearrange("p t h r -> p t (h r)")
                        wv = wv.unsqueeze(3).broadcast_to([P, T, 2 * R, HD])
                        yield dve, m, picked, combined
                        products = dve.do(lambda e_, i, b=b, wv=wv: e_.tensor_tensor(
                            prod[:, :, :, :, :].rearrange("p t h r d -> p t (h r) d"),
                            bank[b][:, :].rearrange("p (t x d) -> p t x d", t=T, d=HD), wv, ALU.mult),
                            ev("products"), S)
                        banks.give(b, products)
                        yield dve, products
                        combined = dve.do(lambda e_, i, pair=pair: e_.tensor_reduce(
                            att[:, :, 16 * pair:16 * pair + 16].rearrange("p t (h d) -> p t h d", d=HD),
                            prod[:, :, :, :, :].rearrange("p t h r d -> p t h d r"), AX, ALU.add),
                            ev("combined"), S)
                done["all combined"] = combined

            half2 = lambda v: v.rearrange("p (h a d) -> p h a d", a=2, d=DH // 2)
            heads = lambda v: v.rearrange("p (h d) -> p h d", d=DH)
            stage = (x_b, x_mid)
            projecting = Slots(1)
            windows = Slots(NWIN)

            def local():
                taken = dve.do(lambda e, i: e.tensor_copy(x_b[:, :, :], x_fresh[:, :, :]), ev("taken"), S)
                done["taken"] = taken
                for j in range(T):
                    done["x", 0, j] = taken
                for l in range(LAYERS):
                    steps.start(projections(l), RANK_LOCAL)
                    for w in range(2 * T):
                        steps.start(window(l, w), RANK_LOCAL)
                    steps.start(finish(l), RANK_LOCAL)
                yield dve, None

            def projections(l):
                xs = stage[l]
                for j in range(T):
                    yield pe, *(yield from need(("x", l, j)))
                    _, users = yield from projecting.take()
                    b = yield from take()
                    mm(bank[b][0:64, 0:P], xs[:, j, 0:64], ident[:, :], True, True)
                    m = mm(bank[b][64:P, 0:P], xs[:, j, 64:D], later[:, 0, :], True, j == 0, ev("shifted"))
                    if j:
                        m = mm(bank[b][64:P, 0:P], xs[:, j - 1, 64:D], later[:, 1, :], False, True, ev("shifted"))
                    yield act, m, *users
                    hf = A(feat_l[:, :], bank[b][:, 0:P], ACT.Copy, ev("shifted_feat"))
                    banks.give(b, hf)
                    yield pe, hf
                    both = yield from take(2)
                    m = [mm(bank[b][:, :], feat_l[:, :], wqkv[l][:, a * INNER:(a + 1) * INNER], True, True,
                            ev("qk_in")) for a, b in enumerate(both)]
                    for a, b in enumerate(both):
                        yield act, m[a], *users
                        r = A(sq[:, a, :], bank[b][:, :], ACT.Square, ev("squares"))
                    yield dve, r
                    r = dve.do(lambda e, i: e.tensor_reduce(
                        ss[:, :, :], sq[:, :, :].rearrange("p a (h d) -> p a h d", d=DH), AX, ALU.add),
                        ev("sumsq"), 2 * INNER)
                    fs = ss[:, :, :].rearrange("p a h -> p (a h)")
                    fr = rn[:, :, :].rearrange("p a h -> p (a h)")
                    yield pool, r
                    r = pool.do(lambda e, i: e.tensor_scalar(fr, fs, 1e-24, None, ALU.max), ev("rnorm"), 16)
                    yield pool, r
                    r = pool.do(lambda e, i: e.tensor_tensor(fr, fr, neg_half[:, :], ALU.pow), ev("rnorm"), 16)
                    for a, b in enumerate(both):
                        steps.start(rotate(l, j, a, b, r), RANK_LOCAL)
                    yield pe, hf
                    b = yield from take()
                    mv = mm(bank[b][:, :], feat_l[:, :], wqkv[l][:, 2 * INNER:3 * INNER], True, True, ev("v_in"))
                    used = ()
                    if j:
                        used = yield from need(("out", l, 2 * j - 1), ("out", l, 2 * j - 2))
                        used.append(done["v", l, j - 1])
                    yield act, mv, *used
                    vo = A(v_odd[l][:, :], bank[b][:, :], ACT.Copy, ev("v_odd"))
                    banks.give(b, vo)
                    yield sp, vo, *used
                    e = sp.do(lambda e_, i, j=j: e_.dma_start(v_even[l][0:64, j % 2, :], v_odd[l][0:64, :]),
                              ev(f"v_even{l}{j}", 16))
                    if j + 1 < T:
                        e = sp.do(lambda e_, i, j=j: e_.dma_start(v_even[l][64:P, (j + 1) % 2, :],
                                                                  v_odd[l][64:P, :]), ev(f"v_even{l}{j}", 16))
                    done["v", l, j] = e
                    tq, tk = yield from need(("turned", l, j, 0), ("turned", l, j, 1))
                    projecting.give(0, tq, tk, mv)

            def rotate(l, j, a, b, rnorm):
                yield dve, rnorm
                n_ = TT(dve, heads(qn[:, a, :]), heads(bank[b][:, :]),
                        rn[:, a, :].unsqueeze(2).broadcast_to([P, NH, DH]), ALU.mult, ev("qk_normed"))
                banks.give(b, n_)
                yield pool, n_
                r1 = TT(pool, heads(q_rot[:, a, :]), heads(qn[:, a, :]),
                        rot[l][:, 2 * a, j, :].unsqueeze(1).broadcast_to([P, NH, DH]), ALU.mult, ev("rot_cos"))
                yield dve, n_
                v, w = half2(qn[:, a, :]), half2(rot_sin[:, a, :])
                for u in range(2):
                    sn = rot[l][:, 2 * a + 1, j, 32 * u:32 * u + 32]
                    r2 = TT(dve, w[:, :, u, :], v[:, :, 1 - u, :],
                            sn.unsqueeze(1).broadcast_to([P, NH, 32]), ALU.mult, ev("rot_sin"))
                yield dve, r1, r2
                r = TT(dve, q_rot[:, a, :], q_rot[:, a, :], rot_sin[:, a, :], ALU.add, ev("rotated"))
                yield pe, r
                b = yield from take()
                for c in range(PAIRS):
                    m = transpose(bank[b][:, c * P:(c + 1) * P], q_rot[:, a, c * P:(c + 1) * P],
                                  ev("qk_turned") if c == PAIRS - 1 else None)
                done["turned", l, j, a] = m
                used = ()
                if j:
                    used = yield from need(("scored", l, 2 * j - 1), ("scored", l, 2 * j - 2))
                if a == 0:
                    yield act, m, *used
                    for u in range(2):
                        v = bank[b][64 * u:64 * u + 64, :].rearrange("p (c w n) -> p c w n", c=PAIRS, w=2)
                        r = A(q_diag[l][64 * u:64 * u + 64, :, :, 64 * u:64 * u + 64], v, ACT.Copy, ev("q_diag"))
                else:
                    yield dve, m, *used
                    r = dve.do(lambda e_, i: e_.tensor_copy(
                        k_ring[l][:, :, (j % 2) * P:(j % 2) * P + P],
                        bank[b][:, :].rearrange("p (c n) -> p c n", c=PAIRS)), ev("k_feat"), S)
                banks.give(b, r)
                done["qk"[a], l, j] = r

            def window(l, w):
                j, odd = divmod(w, 2)
                yield pe, *(yield from need(("q", l, j), ("k", l, j)))
                n, users = yield from windows.take()
                b = yield from take()
                mm(bank[b][:, :].rearrange("p (c n) -> p c n", c=PAIRS), identb[:, :],
                   mask[:, 0 if odd else 2 if w == 0 else 1, :].unsqueeze(1).broadcast_to([P, PAIRS, P]),
                   True, False)
                for c in range(PAIRS):
                    keys = k_ring[l][:, c, :].rearrange("p (a n) -> p a n", n=WIN)
                    if odd:
                        keys = keys[:, 2 * (j % 2):2 * (j % 2) + 2, :]
                    elif w:
                        keys = keys[:, 0:4:3, :] if j % 2 == 0 else keys[:, 2:0:-1, :]
                    else:
                        keys = keys[:, 0:1, :].broadcast_to([P, 2, WIN])
                    m = mm(bank[b][:, c * P:(c + 1) * P].rearrange("p (a n) -> p a n", a=2),
                           q_diag[l][:, c, odd, :], keys, False, c == PAIRS - 1,
                           ev("w_scores") if c == PAIRS - 1 else None)
                done["scored", l, w] = m
                v = bank[b][:, :].rearrange("p (c k) -> p c k", c=PAIRS)
                yield dve, m, *users
                r = dve.do(lambda e_, i: e_.tensor_reduce(wmax[:, n, :], v, AX, ALU.max, negate=True),
                           ev("w_max"), S)
                yield act, r, *users
                for c in range(PAIRS):
                    r = A(pw[:, n, c, :], v[:, c, :], ACT.Exp, ev("w_exp"), bias=wmax[:, n, c:c + 1],
                          accum_out=wsum[:, n, c:c + 1])
                banks.give(b, r)
                yield dve, r
                r = dve.do(lambda e_, i: e_.reciprocal(wrec[:, n, :], wsum[:, n, :]), ev("w_rec"), 4)
                yield pool, r
                r = pool.do(lambda e_, i: e_.tensor_tensor(
                    pw[:, n, :, :], pw[:, n, :, :], wrec[:, n, :].unsqueeze(2).broadcast_to([P, PAIRS, P]),
                    ALU.mult), ev("w_norm"), S)
                yield pe, r
                b = yield from take()
                for c in range(PAIRS):
                    m = transpose(bank[b][:, c * P:(c + 1) * P], pw[:, n, c, :],
                                  ev("p_turned") if c == PAIRS - 1 else None)
                src = bank[b][:, :].rearrange("p (c k) -> p c k", c=PAIRS)
                if odd:
                    yield dve, m
                    r = dve.do(lambda e_, i: e_.tensor_copy(pt[:, n, :, :], src), ev("pt_dve"), S)
                else:
                    yield act, m
                    r = A(pt[:, n, :, :], src, ACT.Copy, ev("pt_act"))
                banks.give(b, r)
                vt, = yield from need(("v", l, j))
                yield pe, r, vt, None if odd or not j else done["v", l, j - 1]
                b = yield from take()
                vv = v_odd[l][:, :] if odd else v_even[l][:, j % 2, :]
                rows = slice(0, 64 if w == 0 else P)
                for c in range(PAIRS):
                    m = mm(bank[b][:, c * P:(c + 1) * P], vv[rows, c * P:(c + 1) * P], pt[rows, n, c, :],
                           True, True, ev("w_out") if c == PAIRS - 1 else None)
                done["out", l, w] = m
                windows.give(n, m)
                used = ()
                if j:
                    used = yield from need(("wo", l, j - 1))
                yield act, m, *used
                for u in range(2):
                    r = A(o_feat[l][64 * u:64 * u + 64, :, odd * WIN:(odd + 1) * WIN],
                          bank[b][64 * u:64 * u + 64, :].rearrange("p (c x n) -> p c x n",
                                                                   c=PAIRS, x=2)[:, :, u, :],
                          ACT.Copy, ev("o_feat"))
                banks.give(b, r)
                done["o", l, w] = r

            def finish(l):
                buf, xs, y = tail[l], stage[l], x_att[l]
                one = dict(stats=buf["stats"][:, :].unsqueeze(1), moments=buf["moments"][:, :].unsqueeze(1),
                           rstd=buf["rstd"])
                L, c0 = f"l{l}_", 8 + 8 * l
                for j in range(T):
                    yield pe, *(yield from need(("o", l, 2 * j), ("o", l, 2 * j + 1)))
                    b = yield from take()
                    for c in range(PAIRS):
                        m = mm(bank[b][:, 0:P], o_feat[l][:, c, :], wo[l][:, c, :], c == 0, c == PAIRS - 1,
                               ev("wo") if c == PAIRS - 1 else None)
                    done["wo", l, j] = m
                    yield dve, m
                    ya = TT(dve, y[:, j, :], bank[b][:, 0:P], xs[:, j, :], ALU.add, ev("res_att"))
                    banks.give(b, ya)
                    yield pool, ya, done.get(("sum used", l))
                    rs = TT(pool, buf["sum"][:, :], y[:, j, :], bias_2[l][:, :], ALU.add, ev("tail_sum"))
                    if l == LAYERS - 1:
                        yield pool, rs
                        rs = TT(pool, buf["sum"][:, :], buf["sum"][:, :], x_b[:, j, :], ALU.add, ev("tail_sum"))
                    yield pe, ya
                    b = yield from take()
                    mm(bank[b][:, 0:64], ident[:, :], y[:, j, 0:64], True, True)
                    m = mm(bank[b][:, 64:D], later[:, 0, :], y[:, j, 64:D], True, j == 0, ev("y_shifted"))
                    if j:
                        m = mm(bank[b][:, 64:D], later[:, 1, :], y[:, j - 1, 64:D], False, True, ev("y_shifted"))
                    nn = yield from norm(bank[b][:, 0:P].unsqueeze(1), buf["normed"].unsqueeze(1), 1, one,
                                         L + "ln", m)
                    banks.give(b, nn)
                    yield pe, nn
                    b = yield from take()
                    m = transpose(bank[b][:, 0:P], buf["normed"], ev("n_turned"))
                    yield act, m
                    r = A(buf["feat"], bank[b][:, 0:P], ACT.Identity, ev("affine"),
                          scale=cols[:, c0:c0 + 1], bias=cols[:, c0 + 1:c0 + 2])
                    banks.give(b, r)
                    yield pe, r
                    both = yield from take(2)
                    for half, b in ((1, both[0]), (0, both[1])):
                        for c, (o_, n_) in enumerate(HCH):
                            m = mm(bank[b][0:n_, c * P:(c + 1) * P],
                                   w1[l][:, half * HID + o_:half * HID + o_ + n_], buf["feat"], True, True,
                                   ev("mlp_in") if c == 2 else None)
                        if half:
                            mg = m
                    yield act, mg
                    for c, (o_, n_) in enumerate(HCH):
                        r = A(buf["gate"][0:n_, c, :], bank[both[0]][0:n_, c * P:(c + 1) * P], ACT.Gelu,
                              ev("gelu"), bias=cols[0:n_, c0 + 5 + c:c0 + 6 + c])
                    banks.give(both[0], r)
                    yield dve, r, m
                    for c, (o_, n_) in enumerate(HCH):
                        r = dve.do(lambda e_, i, c=c, n_=n_, b=both[1]: e_.scalar_tensor_tensor(
                            out=buf["hid"][0:n_, c, :], in0=bank[b][0:n_, c * P:(c + 1) * P],
                            scalar=cols[0:n_, c0 + 2 + c:c0 + 3 + c], in1=buf["gate"][0:n_, c, :],
                            op0=ALU.add, op1=ALU.mult), ev("gated"))
                    banks.give(both[1], r)
                    yield pe, r
                    b = yield from take()
                    for c, (o_, n_) in enumerate(HCH):
                        m = mm(bank[b][:, 0:P], buf["hid"][0:n_, c, :], w2[l][0:n_, c, :], c == 0, c == 2,
                               ev("mlp_out") if c == 2 else None)
                    yield dve, m, rs
                    if l < LAYERS - 1:
                        done["x", l + 1, j] = done["sum used", l] = r = TT(
                            dve, stage[l + 1][:, j, :], buf["sum"][:, :], bank[b][:, 0:P], ALU.add, ev("x_next"))
                        banks.give(b, r)
                        continue
                    r = TT(dve, buf["sum"][:, :], buf["sum"][:, :], bank[b][:, 0:P], ALU.add, ev("x_next"))
                    banks.give(b, r)
                    r = done["sum used", l] = yield from norm(
                        buf["sum"][:, :].unsqueeze(1), x_b[:, j:j + 1, :], 1, one, "ln4", r)
                    yield sp, r
                    sp.do(lambda e, i, j=j: e.dma_start(
                        out[i if i is not None else n_batches - 1, j * P:(j + 1) * P], x_b[:, j, :]),
                        ev("stored", 16))

            if with_local:
                steps.start(local(), RANK_LOCAL)
            if with_search:
                steps.start(search(1), RANK_SEARCH)
            steps.run()
            return pe, act, dve, pool, sp

        n_batches = t["x"].shape[0]

        def play(queues, turn=None):
            with nc.Block() as block:
                for queue, decorate in zip(queues, (block.tensor, block.scalar, block.vector, block.gpsimd,
                                                    block.sync)):
                    @decorate
                    def _(eng, queue=queue):
                        queue.play(eng, turn)
                        if queue is queues[-1]:
                            for v in events.values():
                                if v.n:
                                    eng.wait_ge(v.sem, v.n)
            numbers = sorted(v.sem.num for v in events.values())
            assert numbers == list(range(numbers[0], numbers[-1] + 1))
            nc.sync.sem_clear(range(numbers[0], numbers[-1] + 1))
            nc.all_engine_barrier()

        play(setup)
        play(section(True, False))
        if n_batches > 1:
            body = section(True, True)
            with nc.Fori(0, n_batches - 1, 1) as i:
                play(body, i)
        play(section(False, True))


def kernel(**inputs):
    import ml_dtypes
    import concourse.bacc as bacc
    from concourse.bass_utils import run_bass_kernel_spmd

    v = {k.replace("L0_attn_", "").replace("L0_ffn_", "f:"): np.asarray(a) for k, a in inputs.items()}
    col = lambda a: np.ascontiguousarray(a.reshape(-1, 1))
    rowv = lambda a: np.ascontiguousarray(a.reshape(-1))
    f = np.float32
    half = np.arange(0, DH, 2).astype(f)
    inv = (f(1.0) / (f(10000.0) ** (half / f(DH)))).astype(f)
    pos = np.arange(S).astype(f)
    ang = (pos[:, None] * inv[None, :]).astype(f)
    ang = np.concatenate([ang, ang], -1)
    base = (half + f(0.4 * DH)) / f(1.4 * DH)
    power = (pos - S // 2) / f(WIN // 2)
    sc = (base[None, :] ** power[:, None]).astype(f)
    sc = np.concatenate([sc, sc], -1)
    sign = np.where(np.arange(DH) < DH // 2, f(-1), f(1))[None, :]
    cos, sin = np.cos(ang).astype(f), np.sin(ang).astype(f) * sign
    tables = np.stack([cos * sc * f(8.0), sin * sc * f(8.0), cos / sc, sin / sc]).astype(f)
    tables = np.ascontiguousarray(tables.reshape(4, T, P, DH).transpose(0, 2, 1, 3))
    i = (np.arange(P) % WIN)[:, None]
    jj = np.arange(2 * WIN)[None, :]
    bad = (jj > WIN + i) | (jj < i)
    swap = lambda m: np.concatenate([m[:, WIN:], m[:, :WIN]], 1)
    masks = [bad, swap(bad), swap(bad | (jj < WIN))]
    mask = np.stack([np.where(m, f(MASKED), f(0)) for m in masks], 1)
    arrays = {
        "x": v["x"], "ident": np.eye(P, dtype=f), "identb": np.eye(P).astype(ml_dtypes.bfloat16),
        "later": np.ascontiguousarray(np.stack([np.eye(P, k=1), np.eye(P, k=1 - P)], 1).astype(f)),
        "mask": np.ascontiguousarray(mask.astype(ml_dtypes.bfloat16)), "tables": tables,
        "WqT": np.ascontiguousarray(v["Wq"].T), "WkT": np.ascontiguousarray(v["Wk"].T),
        "WvT": np.ascontiguousarray(v["Wv"].T), "WqvT": np.ascontiguousarray(v["Wqv"].T),
        "WfT": np.ascontiguousarray(v["Wf"].T), "Wr1T": np.ascontiguousarray(v["Wr1"].T),
        "Wr2T": np.ascontiguousarray(v["Wr2"].T.reshape(2, P, D).transpose(1, 0, 2)),
        "bv": rowv(v["bv"]), "bqv": rowv(v["bqv"]), "bf": rowv(v["bf"]), "br2": rowv(v["br2"]),
        "bq": col(v["bq"]), "bk": col(v["bk"]), "g1": col(v["g1"]), "b1": col(v["b1"]),
        "g2": col(v["g2"]), "b2": col(v["b2"]), "br1": np.ascontiguousarray(v["br1"].reshape(2, P).T),
        "Ws": rowv(v["Ws"]), "bs": v["bs"],
        "wqkv": v["f:wqkv"], "wo": v["f:wo"], "w1": v["f:w1"], "w2": v["f:w2"],
        "fb2": v["f:b2"].reshape(LAYERS, D), "fb1": v["f:b1"].reshape(LAYERS, 2 * HID, 1),
        "ln_g": v["f:ln_g"].reshape(LAYERS, D, 1), "ln_b": v["f:ln_b"].reshape(LAYERS, D, 1),
        "q_scale": v["f:q_scale"].reshape(LAYERS, DH), "k_scale": v["f:k_scale"].reshape(LAYERS, DH),
    }
    arrays = {"in_" + k: np.ascontiguousarray(a) for k, a in arrays.items()}
    nc = bacc.Bacc("TRN2", target_bir_lowering=False, num_devices=1)
    tensors = {k[3:]: nc.dram_tensor(k, list(a.shape), mybir.dt.from_np(a.dtype), kind="ExternalInput").ap()
               for k, a in arrays.items()}
    out = nc.dram_tensor("out_0", list(v["x"].shape), F32, kind="ExternalOutput").ap()
    build(nc, tensors, out)
    r = run_bass_kernel_spmd(nc, [arrays], core_ids=[0])
    return r.results[0]["out_0"]
```

```python
from contextlib import ExitStack

import numpy as np

import concourse.bass as bass
from concourse import mybir

F32 = mybir.dt.float32
BF16 = mybir.dt.bfloat16
ALU = mybir.AluOpType
ACT = mybir.ActivationFunctionType
AX = mybir.AxisListType.X

P = 128
B, S, D = 8, 512, 128
T = S // P
EPS = 1e-5

H, HD = 16, 8
R = 8
QK = 32
RV = R * HD
QUADS = H // 4
VC = 96
SPLIT = 3
NPROD = SPLIT * SPLIT * HD
GUARD = 96

LAYERS = 2
NH, DH = 8, 64
INNER = NH * DH
WIN = 64
PAIRS = NH // 2
HID = 341
HCH = [(0, 114), (114, 114), (228, HID - 228)]
MASKED = -3.0e38


class Event:

    def __init__(self, sem, step):
        self.sem, self.step, self.n = sem, step, 0


class Tick:

    def __init__(self, event, n, time):
        self.event, self.n, self.time = event, n, time


class Queue:

    def __init__(self, fixed, column, landing):
        self.items, self.now = [], 0.0
        self.fixed, self.column, self.landing = fixed, column, landing

    def do(self, make, event=None, columns=P):
        self.items.append((make, event))
        self.now += self.fixed + columns * self.column
        if event is None:
            return None
        event.n += event.step
        return Tick(event, event.n, self.now + self.landing)

    def wait(self, *ticks):
        for x in ticks:
            if x is not None:
                self.items.append((None, x))
                self.now = max(self.now, x.time)

    def then(self, make, event, columns=P):
        t = self.do(make, event, columns)
        self.wait(t)
        return t

    def play(self, eng, turn):
        for make, x in self.items:
            if make is None:
                eng.wait_ge(x.event.sem, x.n)
            else:
                ins = make(eng, turn)
                if x is not None:
                    ins.then_inc(x.sem, x.step)


class Slots:

    def __init__(self, n):
        self.idle = {i: () for i in range(n)}

    def take(self, n=1):
        yield lambda: len(self.idle) >= n
        since = lambda i: (max([x.time for x in self.idle[i]], default=0.0), i)
        got = sorted(self.idle, key=since)[:n]
        ticks = [x for i in got for x in self.idle.pop(i)]
        return (got[0] if n == 1 else got), ticks

    def give(self, i, *ticks):
        self.idle[i] = ticks


RANK_LOCAL, RANK_SEARCH = 0.4, 0.0
MAXIMA, EXPS = 1, 1


class Steps:

    def __init__(self):
        self.processes = []

    def start(self, process, rank=0):
        self.processes.append([process, next(process), rank])

    def run(self):
        while self.processes:
            best = None
            for p in self.processes:
                want = p[1]
                if callable(want):
                    if not want():
                        continue
                    key = (-1.0, p[2])
                else:
                    ready = max([x.time for x in want[1:] if x is not None], default=0.0)
                    key = (max(want[0].now, ready), ready + p[2])
                if best is None or key < best[0]:
                    best = key, p
            p = best[1]
            if not callable(p[1]):
                p[1][0].wait(*p[1][1:])
            try:
                p[1] = next(p[0])
            except StopIteration:
                self.processes.remove(p)


def build(nc, t, out):
    ctx = ExitStack()
    with ctx:
        def sb(name, shape, dt=F32):
            return ctx.enter_context(nc.sbuf_tensor(name, shape, dt))

        events = {}

        def ev(name, step=1):
            if name not in events:
                events[name] = Event(ctx.enter_context(nc.semaphore(name)), step)
            return events[name]

        bank = [ctx.enter_context(nc.psum_tensor(f"bank{i}", [P, 512], F32)) for i in range(8)]

        ident = sb("ident", [P, P])
        identb = sb("identb", [P, P], BF16)
        neg_half = sb("neg_half", [P, 2 * NH])
        later = sb("later", [P, 2, P])
        w_all = sb("w_all", [P, 7 * D + VC])
        wq, wk, wf, wr1 = w_all[:, 0:D], w_all[:, D:2 * D], w_all[:, 2 * D:3 * D], w_all[:, 3 * D:5 * D]
        wr2 = w_all[:, 5 * D:7 * D].rearrange("p (c n) -> p c n", c=2)
        wv_all = w_all[:, 7 * D:7 * D + VC]
        cols = sb("cols", [P, 24])
        rows = sb("rows", [P, 4 * D + HD + QK + 1])
        bias_f, bias_r2 = rows[:, 0:D], rows[:, D:2 * D]
        bias_2 = [rows[:, (2 + l) * D:(3 + l) * D] for l in range(LAYERS)]
        ws, bs = rows[:, 4 * D:4 * D + HD + QK], rows[:, 4 * D + HD + QK:4 * D + HD + QK + 1]
        bias_v = sb("bias_v", [P, VC])
        wqkv = [sb(f"wqkv{l}", [P, 3 * INNER]) for l in range(LAYERS)]
        wo = [sb(f"wo{l}", [P, PAIRS, D]) for l in range(LAYERS)]
        w1 = [sb(f"w1_{l}", [P, 2 * HID]) for l in range(LAYERS)]
        w2 = [sb(f"w2_{l}", [P, 3, D]) for l in range(LAYERS)]
        rot = [sb(f"rot{l}", [P, 4, T, DH]) for l in range(LAYERS)]
        mask = sb("mask", [P, 3, P], BF16)

        x_fresh = sb("x_fresh", [P, T, D])
        x_in = x_fresh
        norm_s = dict(stats=sb("stats_s", [P, T, 6]),
                      moments=sb("moments_s", [P, T, 2]), rstd=sb("rstd_s", [P, T]))
        qs = sb("q_stack", [P, H, S], BF16)
        ks = sb("k_stack", [P, H, S], BF16)
        v_tok = sb("v_tok", [P, T, VC])
        pick_q = sb("pick_q", [P, T, H])
        rowmax = sb("rowmax", [P, 2, 16])
        negmax = sb("negmax", [16, 2, 2, P], BF16)
        NPROBS = 5
        probs = sb("probs", [P, NPROBS, T, S])
        NRAW = 3
        raw = sb("raw", [P, NRAW, S])
        EARLY = (3 * QUADS - 1) % NPROBS
        place = [probs[:, n, :, :].rearrange("p t s -> p (t s)") for n in range(NPROBS)]
        at = [0] * NPROBS

        def over(n, size):
            at[n] += size
            return place[n][:, at[n] - size:at[n]]

        a, b, c = EARLY, (EARLY + 1) % NPROBS, (EARLY + 2) % NPROBS
        prep = dict(x=over(a, T * D).rearrange("p (t d) -> p t d", t=T),
                    normed=over(a, T * D).rearrange("p (t d) -> p t d", t=T), feat=over(a, S),
                    stats=over(a, T * 6).rearrange("p (t c) -> p t c", t=T),
                    moments=over(a, T * 2).rearrange("p (t c) -> p t c", t=T), rstd=over(a, T),
                    whole=over(b, 2 * S).rearrange("p (a s) -> p a s", a=2),
                    rest=over(b, 2 * S).rearrange("p (a s) -> p a s", a=2),
                    parts=[over(c, SPLIT * S // 2).bitcast(BF16).rearrange("p (c s) -> p c s", c=SPLIT)
                           for _ in range(2)])
        small = sb("small", [P, S])
        rden = sb("rden", [P, T, 4]); logit = sb("logit", [P, T, 4, R]); lmax = sb("lmax", [P, T, 4])
        lexp = sb("lexp", [P, T, 4, R]); lsum = sb("lsum", [P, T, 4]); lrec = sb("lrec", [P, T, 4])
        weight = sb("weight", [P, T, 4, R])
        prod = sb("prod", [P, T, 2, R, HD])
        att = sb("att", [P, T, D])
        norm_s["normed"] = raw[:, 2, :].rearrange("p (t d) -> p t d", t=T)
        feat_s = small
        hid_s = raw

        x_b = sb("x_b", [P, T, D])
        x_mid = sb("x_mid", [P, T, D])
        x_att = [sb(f"x_att{l}", [P, T, D]) for l in range(LAYERS)]
        feat_l = sb("feat_l", [P, 2, P])
        NWORK = 3
        work = sb("work", [P, NWORK, 2, INNER])
        work_ss = sb("work_ss", [P, NWORK, NH]); work_rn = sb("work_rn", [P, NWORK, NH])
        q_diag = [sb(f"q_diag{l}", [P, PAIRS, 2, P]) for l in range(LAYERS)]
        k_ring = [sb(f"k_ring{l}", [P, PAIRS, 2 * P]) for l in range(LAYERS)]
        v_odd = [sb(f"v_odd{l}", [P, 2, INNER]) for l in range(LAYERS)]
        v_even = [sb(f"v_even{l}", [P, 2, INNER]) for l in range(LAYERS)]
        o_feat = [sb(f"o_feat{l}", [P, PAIRS, P]) for l in range(LAYERS)]
        NWIN = 3
        wmax = sb("wmax", [P, NWIN, PAIRS]); wsum = sb("wsum", [P, NWIN, PAIRS])
        wrec = sb("wrec", [P, NWIN, PAIRS])
        pw = sb("pw", [P, NWIN, PAIRS, P]); pt = pw
        NTAIL = 3
        tail = [dict(stats=sb(f"tail_stats{n}", [P, 1, 6]), moments=sb(f"tail_moments{n}", [P, 1, 2]),
                     rstd=sb(f"tail_rstd{n}", [P, 1]), gate=sb(f"gate{n}", [P, 3, P]),
                     hid=sb(f"hid{n}", [P, 3, P]), sum=sb(f"tail_sum{n}", [P, P])) for n in range(NTAIL)]
        for buf in tail:
            buf["normed"], buf["feat"] = buf["gate"][:, 0, :], buf["hid"][:, 0, :]

        scratch = nc.dram_tensor("parts_scratch", [2, SPLIT, HD, H, S], BF16, kind="Internal").ap()

        def queues():
            return (Queue(0.01, 0.0018, 0.05), Queue(0.11, 0.0008, 0.1),
                    Queue(0.07, 0.00105, 0.25), Queue(0.2, 0.002, 0.1),
                    Queue(0.1, 0.003, 2.0))

        pe, act, dve, pool, sp = queues()
        s_load, s_dve, s_pool = ev("setup_load", 16), ev("setup_dve"), ev("setup_pool")
        flat = probs[:, 4, :, :].rearrange("p t s -> p (t s)")
        wqv_tmp, bqv_tmp, fold_tmp = flat[:, 0:512], flat[:, 512:1024], flat[:, 1024:1536]
        tab = probs[:, 3, 0:2, :].rearrange("p a (b t d) -> p (a b) t d", t=T, d=DH)
        scl = probs[:, 3, 2, 0:4 * LAYERS * DH].rearrange("p (l c d) -> p l c d", l=LAYERS, c=4)
        stack = lambda x: x.rearrange("p h n -> p (h n)")
        loads = [
            (wqv_tmp, t["WqvT"]), (w_all[:, :], t["w_all"]), (cols[:, :], t["cols"]),
            (rows[:, :], t["rows"].partition_broadcast(P)), (bias_v[:, 0:RV], t["bv"].partition_broadcast(P)),
            (bqv_tmp, t["bqv"].partition_broadcast(P)), (tab, t["tables"]), (ident[:, :], t["ident"]),
            (probs[:, 3, 2, 0:4 * LAYERS * DH], t["scales"].partition_broadcast(P)),
            (stack(ks[NPROD:GUARD + 2, :, :]), t["under"]),
            (stack(qs[NPROD:GUARD, :, :]), t["under"][0:GUARD - NPROD]),
        ]
        for n, (dst, src) in enumerate(loads):
            loaded = (sp, act)[n % 2].do(lambda e, i, dst=dst, src=src: e.dma_start(dst, src), s_load)
        for dst, val in [(neg_half[:, :], -0.5), (bias_v[:, RV:VC], 0.0), (q_diag[0][:, :, :, :], 0.0),
                         (q_diag[1][:, :, :, :], 0.0)]:
            pool.then(lambda e_, i, dst=dst, val=val: e_.memset(dst, val), s_pool)
        dve.wait(loaded, Tick(s_pool, s_pool.n, pool.now))

        def fold(src, n, width, part, dst):
            view = src.rearrange("p (g w) -> p g w", w=width)
            tmp = fold_tmp[:, 0:n * width].rearrange("p (g w) -> p g w", w=width)
            coef = ws[:, part:part + width].unsqueeze(1).broadcast_to([P, n, width])
            dve.then(lambda e, i: e.tensor_tensor(tmp, view, coef, ALU.mult), s_dve)
            dve.then(lambda e, i: e.tensor_reduce(dst, tmp, AX, ALU.add), s_dve)

        o = RV + R
        fold(wv_all[:, 0:RV], R, HD, QK, wv_all[:, RV:o])
        fold(bias_v[:, 0:RV], R, HD, QK, bias_v[:, RV:o])
        fold(wqv_tmp, H, QK, 0, wv_all[:, o:o + H])
        fold(bqv_tmp, H, QK, 0, bias_v[:, o:o + H])
        for w in (wv_all, bias_v):
            dve.then(lambda e, i, w=w: e.tensor_scalar(w[:, o:o + H], w[:, o:o + H], float(QK) ** -0.5, None,
                                                       ALU.mult), s_dve)
        dve.then(lambda e, i: e.tensor_scalar(bias_v[:, o:o + H], bias_v[:, o:o + H], bs[:, 0:1], None, ALU.add),
                 s_dve)
        dve.then(lambda e, i: e.tensor_tensor(bias_r2[:, :], bias_r2[:, :], bias_f[:, :], ALU.subtract), s_dve)
        for l in range(LAYERS):
            for c in range(4):
                dve.then(lambda e, i, c=c, l=l: e.tensor_tensor(
                    rot[l][:, c, :, :], tab[:, c, :, :], scl[:, l, c, :].unsqueeze(1).broadcast_to([P, T, DH]),
                    ALU.mult), s_dve)
        setup = (pe, act, dve, pool, sp)

        layer_loads = [(identb[:, :], t["identb"]), (mask[:, :, :], t["mask"]), (later[:, :, :], t["later"])]
        for l in range(LAYERS):
            layer_loads += [(wqkv[l][:, :], t["wqkv"][l]), (w1[l][:, :], t["w1"][l]),
                            (wo[l][:, :, :], t["wo"][l].rearrange("(c p) n -> p c n", p=P))]
            layer_loads += [(w2[l][0:n, c, :], t["w2"][l, o:o + n]) for c, (o, n) in enumerate(HCH)]

        def section(base, with_local=False, with_search=False, with_prepare=False):
            batch = lambda i, k: (base if i is None else i) + k
            for v in events.values():
                v.n = 0
            pe, act, dve, pool, sp = queues()
            steps = Steps()
            banks = Slots(8)
            done = {}

            def need(*keys):
                yield lambda: all(k in done for k in keys)
                return [done[k] for k in keys]

            def take(n=1):
                got, readers = yield from banks.take(n)
                yield pe, *readers
                return got

            def mm(b_out, lhsT, rhs, start, stop, event=None):
                n = 1
                for x in rhs.shape[1:]:
                    n *= x
                n = n // 4 if rhs.dtype == BF16 else n // max(1, P // max(lhsT.shape[1], 32))
                return pe.do(lambda e, i: e.matmul(b_out, lhsT, rhs, start=start, stop=stop,
                                                   skip_group_check=True), event, n)

            def transpose(dst, src, event=None):
                return pe.do(lambda e, i: e.transpose(dst, src, ident[:, :]), event, 60)

            def size(a):
                n = 1
                for x in a.shape[1:]:
                    n *= x
                return n

            def A(dst, src, fn, event, **kw):
                return act.do(lambda e, i: e.activation(dst, src, fn, **kw), event, size(dst))

            def TT(q, dst, a, b, op, event):
                return q.do(lambda e, i: e.tensor_tensor(dst, a, b, op), event, size(dst))

            def norm(src, dst, n, buf, tag, src_ready):
                stats, moments, rstd = buf["stats"], buf["moments"], buf["rstd"]
                yield dve, src_ready
                for j in range(n):
                    x = dve.do(lambda e, i, j=j: e.bn_stats(stats[:, j, :], src[:, j, :]), ev(f"{tag}_stats"))
                yield dve, x
                for j in range(n):
                    x = dve.do(lambda e, i, j=j: e.bn_aggr(moments[:, j, :], stats[:, j, :]),
                               ev(f"{tag}_moments"), 16)
                yield pool, x
                r = pool.do(lambda e, i: e.tensor_scalar(rstd, moments[:, :, 1], EPS, None, ALU.add),
                            ev(f"{tag}_rstd"), n)
                yield pool, r
                r = pool.do(lambda e, i: e.tensor_tensor(rstd, rstd, neg_half[:, 0:n], ALU.pow),
                            ev(f"{tag}_rstd"), n)
                yield dve, r, x
                for j in range(n):
                    last = dve.do(lambda e, i, j=j: e.tensor_scalar(
                        dst[:, j, :], src[:, j, :], moments[:, j, 0:1], rstd[:, j:j + 1],
                        ALU.subtract, ALU.mult), ev(f"{tag}_normed"))
                return last

            def to_feat(src, tag, src_ready):
                yield pe, src_ready
                b = yield from take()
                for j in range(T):
                    last = transpose(bank[b][:, j * P:(j + 1) * P], src[:, j, :],
                                     ev(f"{tag}_turned") if j == T - 1 else None)
                return b, last

            tiles = lambda b: bank[b][:, :].rearrange("p (t d) -> p t d", t=T)
            row = lambda a: a[:, :].unsqueeze(1).broadcast_to([P, T, D])

            def prepare(offset):
                used = ()
                if with_search:
                    used = yield from need(("used", 2 * QUADS - 3), ("small", QUADS - 2))
                yield sp, *used
                x_ld = sp.do(lambda e, i: e.dma_start(
                    prep["x"], t["x"][batch(i, offset)].rearrange("(t p) d -> p t d", p=P)),
                    ev("prep_loaded", 16))
                yield dve, *used
                n1 = yield from norm(prep["x"], prep["normed"], T, prep, "ln1", x_ld)
                b, tf = yield from to_feat(prep["normed"], "ln1", n1)
                yield act, tf
                xf = A(prep["feat"], bank[b][:, :], ACT.Identity, ev("ln1_affine"),
                       scale=cols[:, 2:3], bias=cols[:, 3:4])
                banks.give(b, xf)
                if with_search:
                    used = yield from need(("used", 2 * QUADS - 1), ("small", QUADS - 1))
                for a in range(2):
                    steps.start(split(a, xf, used), RANK_SEARCH)
                yield pe, xf
                b = yield from take()
                for j in range(T):
                    m = mm(bank[b][:, j * VC:(j + 1) * VC], prep["feat"][:, j * P:(j + 1) * P], wv_all[:, :],
                           True, True, ev("v_proj") if j == T - 1 else None)
                yield dve, m, *used
                bv = dve.do(lambda e, i: e.tensor_tensor(
                    v_tok[:, :, :], bank[b][:, 0:T * VC].rearrange("p (t c) -> p t c", t=T),
                    bias_v[:, :].unsqueeze(1).broadcast_to([P, T, VC]), ALU.add), ev("v_biased"), T * VC)
                banks.give(b, bv)
                picked = (yield from need(("picked", QUADS - 1))) if with_search else ()
                yield pool, bv, *picked
                pool.then(lambda e, i: e.tensor_copy(pick_q[:, :, :], v_tok[:, :, RV + R:RV + R + H]),
                          ev("v_ones"))
                pool.then(lambda e, i: e.memset(v_tok[:, :, RV + R:VC], 0.0), ev("v_ones"))
                pool.do(lambda e, i: e.memset(v_tok[:, :, RV + R:RV + R + 1], 1.0), ev("v_ones"))

            def split(a, xf, used):
                yield pe, xf
                b = yield from take()
                m = mm(bank[b][:, :], (wq, wk)[a][:, :], prep["feat"], True, True, ev("qk_proj"))
                s = float(HD) ** -0.5 if a == 0 else 1.0
                whole, rest, parts = prep["whole"][:, a, :], prep["rest"][:, a, :], prep["parts"][a]
                e = ev("split")
                yield dve, m, *used
                r = dve.do(lambda e_, i: e_.tensor_scalar(whole, bank[b][:, :], cols[:, a:a + 1], s, ALU.add,
                                                          ALU.mult), e, S)
                banks.give(b, r)
                def send(c):
                    return sp.do(lambda e_, i: e_.dma_start(scratch[a, c].rearrange("d h n -> h d n"),
                                                            parts[:, c, :]), ev(f"to_scratch{a}", 16))

                for c in range(SPLIT - 1):
                    yield dve, r
                    r = dve.do(lambda e_, i, c=c: e_.tensor_copy(parts[:, c, :], rest if c else whole), e, S)
                    yield sp, r
                    send(c)
                    yield dve, r
                    r = dve.do(lambda e_, i, c=c: e_.tensor_tensor(
                        parts[:, 2, :] if c else rest, rest if c else whole, parts[:, c, :], ALU.subtract), e, S)
                yield sp, r
                yield sp, send(SPLIT - 1)
                for u in range(SPLIT):
                    r0 = u * SPLIT * HD
                    src = scratch[a] if a else scratch[a, u:u + 1].broadcast_to([SPLIT, HD, H, S])
                    src = src.rearrange("c d h n -> c d (h n)")
                    sp.do(lambda e_, i, r0=r0, src=src: e_.dma_start(
                        (qs, ks)[a][r0:r0 + SPLIT * HD, :, :].rearrange("p h n -> p (h n)"), src),
                        ev(f"stacked{a}", 16))

            def search(offset):
                if with_local:
                    yield sp, *(yield from need("taken"))
                done["x"] = sp.do(lambda e, i: e.dma_start(
                    x_in[:, :, :], t["x"][batch(i, offset)].rearrange("(t p) d -> p t d", p=P)),
                    ev("x_loaded", 16))
                pool.wait(done["x"])
                done["x"] = TT(pool, x_in[:, :, :], x_in[:, :, :], row(bias_f), ALU.add, ev("x_biased"))
                for first in range(MAXIMA):
                    steps.start(row_maxima(range(first, T, MAXIMA)), RANK_SEARCH)
                for g in range(QUADS):
                    steps.start(guard(g), RANK_SEARCH)
                for first in range(EXPS):
                    steps.start(exponentials(range(first, T, EXPS)), RANK_SEARCH)
                for x in (values(), retrieval()):
                    steps.start(x, RANK_SEARCH)
                yield from need("all combined")
                for j in range(T):
                    steps.start(search_tail(j), RANK_SEARCH)

            def search_tail(j):
                cut = slice(j * P, (j + 1) * P)
                buf = dict(stats=norm_s["stats"][:, j:j + 1, :], moments=norm_s["moments"][:, j:j + 1, :],
                           rstd=norm_s["rstd"][:, j:j + 1])
                normed, hid = norm_s["normed"][:, j:j + 1, :], hid_s[:, 0:2, cut]
                x_s, x_0 = att[:, j, :], x_in[:, j, :]
                yield pe, done["all combined"]
                b = yield from take()
                m = transpose(bank[b][:, 0:P], x_s, ev("tail_turned"))
                yield act, m
                r = A(feat_s[:, cut], bank[b][:, 0:P], ACT.Copy, ev("tail_feat"))
                banks.give(b, r)
                yield pe, r
                b = yield from take()
                m = mm(bank[b][:, 0:P], feat_s[:, cut], wf[:, :], True, True, ev("wf"))
                yield dve, m, done["x"]
                r = TT(dve, x_s, bank[b][:, 0:P], x_0, ALU.add, ev("res2"))
                banks.give(b, r)
                n2 = yield from norm(att[:, j:j + 1, :], normed, 1, buf, "ln2", r)
                pool.wait(n2, done["x"])
                r = TT(pool, x_s, x_s, x_0, ALU.add, ev("res2_pool"))
                yield pe, n2
                b = yield from take()
                m = transpose(bank[b][:, 0:P], normed[:, 0, :], ev("tail_turned"))
                yield pool, r
                res3 = TT(pool, x_s, x_s, bias_r2[:, :], ALU.add, ev("res2_pool"))
                yield act, m
                r = A(feat_s[:, cut], bank[b][:, 0:P], ACT.Identity, ev("tail_feat"),
                      scale=cols[:, 4:5], bias=cols[:, 5:6])
                banks.give(b, r)
                yield pe, r
                b = yield from take()
                for c in range(2):
                    m = mm(bank[b][:, c * P:(c + 1) * P], wr1[:, c * P:(c + 1) * P], feat_s[:, cut], True, True,
                           ev("mlp1"))
                yield act, m
                for c in range(2):
                    r = A(hid[:, c, :], bank[b][:, c * P:(c + 1) * P], ACT.Relu, ev("relu"),
                          bias=cols[:, 6 + c:7 + c])
                banks.give(b, r)
                yield pe, r
                b = yield from take()
                for c in range(2):
                    m = mm(bank[b][:, 0:P], hid[:, c, :], wr2[:, c, :], c == 0, c == 1, ev("mlp2"))
                yield dve, m, res3
                r = TT(dve, x_s, x_s, bank[b][:, 0:P], ALU.add, ev("res2"))
                banks.give(b, r)
                yield dve, res3
                yield from norm(att[:, j:j + 1, :], x_fresh[:, j:j + 1, :], 1, buf, "ln3", r)

            def row_maxima(mine):
                for h in range(H):
                    g, hh = divmod(h, 4)
                    for j in mine:
                        b = yield from take()
                        m = mm(bank[b][:, :], qs[0:GUARD, h, j * P:(j + 1) * P], ks[0:GUARD, h, :], True, True,
                               ev("scores"))
                        turned = None
                        if hh == 0 and j == mine[0] and g >= 2:
                            turned, = yield from need(("max turned", g - 2))
                        yield dve, m, turned
                        c = hh * T + j
                        r = dve.do(lambda e, i, g=g, c=c, b=b: e.tensor_reduce(
                            rowmax[:, g % 2, c:c + 1], bank[b][:, :], AX, ALU.max, negate=True), ev("row_max"),
                            S)
                        banks.give(b, r)
                        done["max", h, j] = r

            def guard(g):
                yield pe, *(yield from need(*[("max", 4 * g + 3, j) for j in range(T)]))
                b = yield from take()
                m = transpose(bank[b][0:16, 0:P], rowmax[:, g % 2, :], ev("max_turned"))
                done["max turned", g] = m
                yield dve, m, *((yield from need(("guard sent", g - 2))) if g >= 2 else ())
                dve.then(lambda e, i: e.tensor_copy(negmax[:, g % 2, 0, :], bank[b][0:16, 0:P]),
                         ev("guard_split"))
                r = dve.do(lambda e, i: e.tensor_tensor(negmax[:, g % 2, 1, :], bank[b][0:16, 0:P],
                                                        negmax[:, g % 2, 0, :], ALU.subtract),
                           ev("guard_split"))
                banks.give(b, r)
                yield sp, r
                for a in range(2):
                    d = sp.do(lambda e, i, a=a: e.dma_start(
                        qs[GUARD + a:GUARD + a + 1, 4 * g:4 * g + 4, :].rearrange("p h n -> p (h n)"),
                        negmax[:, g % 2, a, :]), ev(f"guard_rows{g}", 16))
                done["guard sent", g] = d

            def exponentials(mine):
                for h in range(H):
                    if h % 4 == 0:
                        yield pe, *(yield from need(("guard sent", h // 4)))
                    used = None
                    if h >= NPROBS:
                        used, = yield from need(("small", (h - NPROBS) // 4))
                    for j in mine:
                        b = yield from take()
                        m = mm(bank[b][:, :], ks[0:GUARD + 2, h, j * P:(j + 1) * P], qs[0:GUARD + 2, h, :],
                               True, True, ev("scores_t"))
                        yield act, m, used
                        r = A(probs[:, h % NPROBS, j, :], bank[b][:, :], ACT.Exp, ev("probs"))
                        banks.give(b, r)
                        done["probs", h, j] = r

            def values():
                for g in range(QUADS):
                    if g < QUADS - 1:
                        yield from raw_values(2 * g)
                        yield from raw_values(2 * g + 1)
                        yield from small_values(g)
                    else:
                        yield from raw_values(2 * g)
                        yield from small_values(g)
                        yield from raw_values(2 * g + 1)

            def raw_values(pair):
                b = yield from take()
                for j in range(T):
                    yield pe, *(yield from need(("probs", 2 * pair, j), ("probs", 2 * pair + 1, j)))
                    for hh in range(2):
                        m = mm(bank[b][64 * hh:64 * hh + 64, :], v_tok[:, j, 0:RV],
                               probs[:, (2 * pair + hh) % NPROBS, j, :], j == 0, j == T - 1,
                               ev("raw_values") if j == T - 1 and hh == 1 else None)
                done["used", pair] = m
                turned = None
                if pair >= NRAW:
                    turned, = yield from need(("raw turned", pair - NRAW))
                yield act, m, turned
                r = A(raw[:, pair % NRAW, :], bank[b][:, :], ACT.Copy, ev("raw_out"))
                banks.give(b, r)
                done["raw", pair] = r

            def small_values(g):
                b = yield from take()
                for j in range(T):
                    yield pe, *(yield from need(("probs", 4 * g + 3, j)))
                    for hh in range(4):
                        m = mm(bank[b][32 * hh:32 * hh + 32, :], v_tok[:, j, RV:VC],
                               probs[:, (4 * g + hh) % NPROBS, j, :], j == 0, j == T - 1,
                               ev("small_values") if j == T - 1 and hh == 3 else None)
                done["small", g] = m
                turned = None
                if g:
                    turned, = yield from need(("small turned", g - 1))
                yield act, m, turned
                r = A(small[:, :], bank[b][:, :], ACT.Copy, ev("small_out"))
                banks.give(b, r)
                done["small out", g] = r

            def retrieval():
                wide = lambda a: a[:, :, :].unsqueeze(3).broadcast_to([P, T, 4, R])
                products = combined = None
                for g in range(QUADS):
                    yield pe, *(yield from need(("small out", g)))
                    b = yield from take()
                    for j in range(T):
                        m = transpose(bank[b][:, j * P:(j + 1) * P], small[:, j * P:(j + 1) * P],
                                      ev("small_turned") if j == T - 1 else None)
                    done["small turned", g] = m
                    tok = bank[b][:, :].rearrange("p (t g c) -> p t g c", t=T, g=4)
                    e = ev("pick")
                    yield dve, m
                    r = dve.do(lambda e_, i, tok=tok: e_.reciprocal(rden[:, :, :], tok[:, :, :, R]), e, 16)
                    yield dve, r
                    r = TT(dve, logit[:, :, :, :], tok[:, :, :, 0:R], wide(rden), ALU.mult, e)
                    banks.give(b, r)
                    pq = pick_q[:, :, 4 * g:4 * g + 4].unsqueeze(3).broadcast_to([P, T, 4, R])
                    yield dve, r
                    r = done["picked", g] = TT(dve, logit[:, :, :, :], logit[:, :, :, :], pq, ALU.add, e)
                    yield dve, r
                    r = dve.do(lambda e_, i: e_.tensor_reduce(lmax[:, :, :], logit[:, :, :, :], AX, ALU.max), e)
                    yield dve, r
                    r = TT(dve, logit[:, :, :, :], logit[:, :, :, :], wide(lmax), ALU.subtract, e)
                    yield act, r
                    r = A(lexp[:, :, :, :], logit[:, :, :, :], ACT.Exp, ev("pick_exp"))
                    yield dve, r
                    r = dve.do(lambda e_, i: e_.tensor_reduce(lsum[:, :, :], lexp[:, :, :, :], AX, ALU.add), e)
                    yield dve, r
                    r = dve.do(lambda e_, i: e_.reciprocal(lrec[:, :, :], lsum[:, :, :]), e, 16)
                    yield dve, r
                    r = dve.do(lambda e_, i: e_.tensor_tensor(lrec[:, :, :], lrec[:, :, :], rden[:, :, :],
                                                              ALU.mult), e, 16)
                    yield dve, r, products
                    picked = TT(dve, weight[:, :, :, :], lexp[:, :, :, :], wide(lrec), ALU.mult, e)
                    for half in range(2):
                        pair = 2 * g + half
                        yield pe, *(yield from need(("raw", pair)))
                        b = yield from take()
                        for j in range(T):
                            m = transpose(bank[b][:, j * P:(j + 1) * P], raw[:, pair % NRAW, j * P:(j + 1) * P],
                                          ev("raw_turned") if j == T - 1 else None)
                        done["raw turned", pair] = m
                        wv = weight[:, :, 2 * half:2 * half + 2, :].rearrange("p t h r -> p t (h r)")
                        wv = wv.unsqueeze(3).broadcast_to([P, T, 2 * R, HD])
                        yield dve, m, picked, combined
                        products = dve.do(lambda e_, i, b=b, wv=wv: e_.tensor_tensor(
                            prod[:, :, :, :, :].rearrange("p t h r d -> p t (h r) d"),
                            bank[b][:, :].rearrange("p (t x d) -> p t x d", t=T, d=HD), wv, ALU.mult),
                            ev("products"), S)
                        banks.give(b, products)
                        yield dve, products
                        combined = dve.do(lambda e_, i, pair=pair: e_.tensor_reduce(
                            att[:, :, 16 * pair:16 * pair + 16].rearrange("p t (h d) -> p t h d", d=HD),
                            prod[:, :, :, :, :].rearrange("p t h r d -> p t h d r"), AX, ALU.add),
                            ev("combined"), S)
                done["all combined"] = combined

            half2 = lambda v: v.rearrange("p (h a d) -> p h a d", a=2, d=DH // 2)
            heads = lambda v: v.rearrange("p (h d) -> p h d", d=DH)
            stage = (x_b, x_mid)
            shifted = Slots(2)
            rotating = Slots(NWORK)
            windows = Slots(NWIN)
            tails = Slots(NTAIL)

            def local():
                taken = dve.do(lambda e, i: e.tensor_copy(x_b[:, :, :], x_fresh[:, :, :]), ev("taken"), S)
                done["taken"] = taken
                for j in range(T):
                    done["x", 0, j] = taken
                for l in range(LAYERS):
                    steps.start(projections(l), RANK_LOCAL)
                    for w in range(2 * T):
                        steps.start(window(l, w), RANK_LOCAL)
                    for j in range(T):
                        steps.start(finish(l, j), RANK_LOCAL)
                yield dve, None

            def projections(l):
                xs = stage[l]
                for j in range(T):
                    yield pe, *(yield from need(("x", l, j)))
                    f, users = yield from shifted.take()
                    feat = feat_l[:, f, :]
                    b = yield from take()
                    mm(bank[b][0:64, 0:P], xs[:, j, 0:64], ident[:, :], True, True)
                    m = mm(bank[b][64:P, 0:P], xs[:, j, 64:D], later[:, 0, :], True, j == 0, ev("shifted"))
                    if j:
                        m = mm(bank[b][64:P, 0:P], xs[:, j - 1, 64:D], later[:, 1, :], False, True, ev("shifted"))
                    yield act, m, *users
                    hf = A(feat, bank[b][:, 0:P], ACT.Copy, ev("shifted_feat"))
                    banks.give(b, hf)
                    for a in range(2):
                        steps.start(rotated(l, j, a, feat, hf), RANK_LOCAL)
                    yield pe, hf
                    b = yield from take()
                    mv = mm(bank[b][:, :], feat, wqkv[l][:, 2 * INNER:3 * INNER], True, True, ev("v_in"))
                    used = ()
                    if j >= 2:
                        used = yield from need(("out", l, 2 * j - 3))
                        used.append(done["v", l, j - 2])
                    yield act, mv, *used
                    vo = A(v_odd[l][:, j % 2, :], bank[b][:, :], ACT.Copy, ev("v_odd"))
                    banks.give(b, vo)
                    used = (yield from need(("out", l, 2 * j - 2))) if j else ()
                    yield sp, vo, *used
                    e = sp.do(lambda e_, i, j=j: e_.dma_start(v_even[l][0:64, j % 2, :], v_odd[l][0:64, j % 2, :]),
                              ev(f"v_even{l}{j}", 16))
                    if j + 1 < T:
                        e = sp.do(lambda e_, i, j=j: e_.dma_start(v_even[l][64:P, (j + 1) % 2, :],
                                                                  v_odd[l][64:P, j % 2, :]), ev(f"v_even{l}{j}", 16))
                    done["v", l, j] = e
                    in_ = yield from need(("in", l, j, 0), ("in", l, j, 1))
                    shifted.give(f, mv, *in_)

            def inverse_norm(l, j, a, ss, rn, r):
                yield pool, r
                r = pool.do(lambda e, i: e.tensor_scalar(rn, ss, 1e-24, None, ALU.max), ev("rnorm"), NH)
                yield pool, r
                done["rn", l, j, a] = pool.do(lambda e, i: e.tensor_tensor(rn, rn, neg_half[:, 0:NH], ALU.pow),
                                              ev("rnorm"), NH)

            def rotated(l, j, a, feat, hf):
                yield pe, hf
                n, users = yield from rotating.take()
                x, y = work[:, n, 0, :], work[:, n, 1, :]
                ss, rn = work_ss[:, n, :], work_rn[:, n, :]
                b = yield from take()
                m = done["in", l, j, a] = mm(bank[b][:, :], feat, wqkv[l][:, a * INNER:(a + 1) * INNER], True,
                                             True, ev("qk_in"))
                yield act, m, *users
                r = A(x, bank[b][:, :], ACT.Square, ev("squares"))
                yield dve, r
                r = dve.do(lambda e, i: e.tensor_reduce(ss, heads(x), AX, ALU.add), ev("sumsq"), INNER)
                steps.start(inverse_norm(l, j, a, ss, rn, r), RANK_LOCAL)
                yield dve, None
                v, w = half2(bank[b][:, :]), half2(y)
                for u in range(2):
                    sn = rot[l][:, 2 * a + 1, j, 32 * u:32 * u + 32]
                    r2 = TT(dve, w[:, :, u, :], v[:, :, 1 - u, :],
                            sn.unsqueeze(1).broadcast_to([P, NH, 32]), ALU.mult, ev("rot_sin"))
                yield dve, r
                r = TT(dve, heads(x), heads(bank[b][:, :]),
                       rot[l][:, 2 * a, j, :].unsqueeze(1).broadcast_to([P, NH, DH]), ALU.mult, ev("rot_cos"))
                banks.give(b, r)
                yield dve, r, r2
                r = TT(dve, x, x, y, ALU.add, ev("rotated"))
                yield pool, r, *(yield from need(("rn", l, j, a)))
                r = TT(pool, heads(x), heads(x), rn.unsqueeze(2).broadcast_to([P, NH, DH]), ALU.mult,
                       ev("qk_normed"))
                used = ()
                if j:
                    used = yield from need(("scored", l, 2 * j - 1), ("scored", l, 2 * j - 2))
                yield pe, r
                b = yield from take()
                for c in range(PAIRS):
                    m = transpose(bank[b][:, c * P:(c + 1) * P], work[:, n, 0, c * P:(c + 1) * P],
                                  ev("qk_turned") if c == PAIRS - 1 else None)
                rotating.give(n, m)
                if a == 0:
                    yield act, m, *used
                    for u in range(2):
                        v = bank[b][64 * u:64 * u + 64, :].rearrange("p (c w n) -> p c w n", c=PAIRS, w=2)
                        r = A(q_diag[l][64 * u:64 * u + 64, :, :, 64 * u:64 * u + 64], v, ACT.Copy, ev("q_diag"))
                else:
                    yield dve, m, *used
                    r = dve.do(lambda e_, i: e_.tensor_copy(
                        k_ring[l][:, :, (j % 2) * P:(j % 2) * P + P],
                        bank[b][:, :].rearrange("p (c n) -> p c n", c=PAIRS)), ev("k_feat"), S)
                banks.give(b, r)
                done["qk"[a], l, j] = r

            def window(l, w):
                j, odd = divmod(w, 2)
                yield pe, *(yield from need(("q", l, j), ("k", l, j)))
                n, users = yield from windows.take()
                b = yield from take()
                mm(bank[b][:, :].rearrange("p (c n) -> p c n", c=PAIRS), identb[:, :],
                   mask[:, 0 if odd else 2 if w == 0 else 1, :].unsqueeze(1).broadcast_to([P, PAIRS, P]),
                   True, False)
                for c in range(PAIRS):
                    keys = k_ring[l][:, c, :].rearrange("p (a n) -> p a n", n=WIN)
                    if odd:
                        keys = keys[:, 2 * (j % 2):2 * (j % 2) + 2, :]
                    elif w:
                        keys = keys[:, 0:4:3, :] if j % 2 == 0 else keys[:, 2:0:-1, :]
                    else:
                        keys = keys[:, 0:1, :].broadcast_to([P, 2, WIN])
                    m = mm(bank[b][:, c * P:(c + 1) * P].rearrange("p (a n) -> p a n", a=2),
                           q_diag[l][:, c, odd, :], keys, False, c == PAIRS - 1,
                           ev("w_scores") if c == PAIRS - 1 else None)
                done["scored", l, w] = m
                v = bank[b][:, :].rearrange("p (c k) -> p c k", c=PAIRS)
                yield dve, m, *users
                r = dve.do(lambda e_, i: e_.tensor_reduce(wmax[:, n, :], v, AX, ALU.max, negate=True),
                           ev("w_max"), S)
                yield act, r, *users
                for c in range(PAIRS):
                    r = A(pw[:, n, c, :], v[:, c, :], ACT.Exp, ev("w_exp"), bias=wmax[:, n, c:c + 1],
                          accum_out=wsum[:, n, c:c + 1])
                banks.give(b, r)
                yield dve, r
                r = dve.do(lambda e_, i: e_.reciprocal(wrec[:, n, :], wsum[:, n, :]), ev("w_rec"), 4)
                yield pool, r
                r = pool.do(lambda e_, i: e_.tensor_tensor(
                    pw[:, n, :, :], pw[:, n, :, :], wrec[:, n, :].unsqueeze(2).broadcast_to([P, PAIRS, P]),
                    ALU.mult), ev("w_norm"), S)
                yield pe, r
                b = yield from take()
                for c in range(PAIRS):
                    m = transpose(bank[b][:, c * P:(c + 1) * P], pw[:, n, c, :],
                                  ev("p_turned") if c == PAIRS - 1 else None)
                src = bank[b][:, :].rearrange("p (c k) -> p c k", c=PAIRS)
                if odd:
                    yield dve, m
                    r = dve.do(lambda e_, i: e_.tensor_copy(pt[:, n, :, :], src), ev("pt_dve"), S)
                else:
                    yield act, m
                    r = A(pt[:, n, :, :], src, ACT.Copy, ev("pt_act"))
                banks.give(b, r)
                vt, = yield from need(("v", l, j))
                yield pe, r, vt, None if odd or not j else done["v", l, j - 1]
                b = yield from take()
                vv = v_odd[l][:, j % 2, :] if odd else v_even[l][:, j % 2, :]
                rows = slice(0, 64 if w == 0 else P)
                for c in range(PAIRS):
                    for u in range(2):
                        m = mm(bank[b][64 * u:64 * u + 64, c * WIN:(c + 1) * WIN],
                               vv[rows, c * P + 64 * u:c * P + 64 * u + 64],
                               pt[rows, n, c, 64 * u:64 * u + 64], True, True,
                               ev("w_out") if c == PAIRS - 1 and u else None)
                done["out", l, w] = m
                windows.give(n, m)
                used = ()
                if j:
                    used = yield from need(("wo", l, j - 1))
                yield act, m, *used
                r = A(o_feat[l][:, :, odd * WIN:(odd + 1) * WIN],
                      bank[b][:, 0:PAIRS * WIN].rearrange("p (c n) -> p c n", c=PAIRS), ACT.Copy, ev("o_feat"))
                banks.give(b, r)
                done["o", l, w] = r

            def finish(l, j):
                xs, y = stage[l], x_att[l]
                L, c0 = f"l{l}_", 8 + 8 * l
                yield pe, *(yield from need(("o", l, 2 * j), ("o", l, 2 * j + 1)))
                n, users = yield from tails.take()
                buf = tail[n]
                one = {k: buf[k][:, :] if k == "rstd" else buf[k][:, :, :] for k in ("stats", "moments", "rstd")}
                b = yield from take()
                for c in range(PAIRS):
                    m = mm(bank[b][:, 0:P], o_feat[l][:, c, :], wo[l][:, c, :], c == 0, c == PAIRS - 1,
                           ev("wo") if c == PAIRS - 1 else None)
                done["wo", l, j] = m
                yield dve, m
                ya = TT(dve, y[:, j, :], bank[b][:, 0:P], xs[:, j, :], ALU.add, ev("res_att"))
                banks.give(b, ya)
                done["y", l, j] = ya
                yield pool, ya, *users
                rs = TT(pool, buf["sum"][:, :], y[:, j, :], bias_2[l][:, :], ALU.add, ev("tail_sum"))
                if l == LAYERS - 1:
                    yield pool, rs
                    rs = TT(pool, buf["sum"][:, :], buf["sum"][:, :], x_b[:, j, :], ALU.add, ev("tail_sum"))
                yield pe, ya, *((yield from need(("y", l, j - 1))) if j else ())
                b = yield from take()
                mm(bank[b][:, 0:64], ident[:, :], y[:, j, 0:64], True, True)
                m = mm(bank[b][:, 64:D], later[:, 0, :], y[:, j, 64:D], True, j == 0, ev("y_shifted"))
                if j:
                    m = mm(bank[b][:, 64:D], later[:, 1, :], y[:, j - 1, 64:D], False, True, ev("y_shifted"))
                nn = yield from norm(bank[b][:, 0:P].unsqueeze(1), buf["normed"].unsqueeze(1), 1, one,
                                     L + "ln", m)
                banks.give(b, nn)
                yield pe, nn
                b = yield from take()
                m = transpose(bank[b][:, 0:P], buf["normed"], ev("n_turned"))
                yield act, m
                r = A(buf["feat"], bank[b][:, 0:P], ACT.Identity, ev("affine"),
                      scale=cols[:, c0:c0 + 1], bias=cols[:, c0 + 1:c0 + 2])
                banks.give(b, r)
                yield pe, r
                both = yield from take(2)
                for half, b in ((1, both[0]), (0, both[1])):
                    for c, (o_, n_) in enumerate(HCH):
                        m = mm(bank[b][0:n_, c * P:(c + 1) * P],
                               w1[l][:, half * HID + o_:half * HID + o_ + n_], buf["feat"], True, True,
                               ev("mlp_in") if c == 2 else None)
                    if half:
                        mg = m
                yield act, mg
                for c, (o_, n_) in enumerate(HCH):
                    r = A(buf["gate"][0:n_, c, :], bank[both[0]][0:n_, c * P:(c + 1) * P], ACT.Gelu,
                          ev("gelu"), bias=cols[0:n_, c0 + 5 + c:c0 + 6 + c])
                banks.give(both[0], r)
                yield dve, r, m
                for c, (o_, n_) in enumerate(HCH):
                    r = dve.do(lambda e_, i, c=c, n_=n_, b=both[1]: e_.scalar_tensor_tensor(
                        out=buf["hid"][0:n_, c, :], in0=bank[b][0:n_, c * P:(c + 1) * P],
                        scalar=cols[0:n_, c0 + 2 + c:c0 + 3 + c], in1=buf["gate"][0:n_, c, :],
                        op0=ALU.add, op1=ALU.mult), ev("gated"))
                banks.give(both[1], r)
                yield pe, r
                b = yield from take()
                for c, (o_, n_) in enumerate(HCH):
                    m = mm(bank[b][:, 0:P], buf["hid"][0:n_, c, :], w2[l][0:n_, c, :], c == 0, c == 2,
                           ev("mlp_out") if c == 2 else None)
                yield dve, m, rs
                if l < LAYERS - 1:
                    done["x", l + 1, j] = r = TT(
                        dve, stage[l + 1][:, j, :], buf["sum"][:, :], bank[b][:, 0:P], ALU.add, ev("x_next"))
                    banks.give(b, r)
                    tails.give(n, r)
                    return
                r = TT(dve, buf["sum"][:, :], buf["sum"][:, :], bank[b][:, 0:P], ALU.add, ev("x_next"))
                banks.give(b, r)
                r = yield from norm(
                    buf["sum"][:, :].unsqueeze(1), x_b[:, j:j + 1, :], 1, one, "ln4", r)
                tails.give(n, r)
                yield sp, r
                sp.do(lambda e, i, j=j: e.dma_start(
                    out[batch(i, 0), j * P:(j + 1) * P], x_b[:, j, :]),
                    ev("stored", 16))

            if with_local:
                steps.start(local(), RANK_LOCAL)
            elif with_search:
                for dst, src in layer_loads:
                    sp.do(lambda e, i, dst=dst, src=src: e.dma_start(dst, src), ev("layer_load", 16))
            if with_search:
                steps.start(search(1), RANK_SEARCH)
            if with_prepare:
                steps.start(prepare(2), RANK_SEARCH)
            steps.run()
            return pe, act, dve, pool, sp

        n_batches = t["x"].shape[0]

        def play(queues, turn=None):
            with nc.Block() as block:
                for queue, decorate in zip(queues, (block.tensor, block.scalar, block.vector, block.gpsimd,
                                                    block.sync)):
                    @decorate
                    def _(eng, queue=queue):
                        queue.play(eng, turn)
                        if queue is queues[-1]:
                            for v in events.values():
                                if v.n:
                                    eng.wait_ge(v.sem, v.n)
            numbers = sorted(v.sem.num for v in events.values())
            assert numbers == list(range(numbers[0], numbers[-1] + 1))
            nc.sync.sem_clear(range(numbers[0], numbers[-1] + 1))
            nc.all_engine_barrier()

        play(setup)
        play(section(-2, with_prepare=True))
        play(section(-1, with_search=True, with_prepare=n_batches > 1))
        if n_batches > 2:
            body = section(None, with_local=True, with_search=True, with_prepare=True)
            with nc.Fori(0, n_batches - 2, 1) as i:
                play(body, i)
        if n_batches > 1:
            play(section(n_batches - 2, with_local=True, with_search=True))
        play(section(n_batches - 1, with_local=True))


def kernel(**inputs):
    import ml_dtypes
    import concourse.bacc as bacc
    from concourse.bass_utils import run_bass_kernel_spmd

    v = {k.replace("L0_attn_", "").replace("L0_ffn_", "f:"): np.asarray(a) for k, a in inputs.items()}
    flat = lambda a: np.reshape(a, -1)
    f = np.float32
    half = np.arange(0, DH, 2).astype(f)
    inv = (f(1.0) / (f(10000.0) ** (half / f(DH)))).astype(f)
    pos = np.arange(S).astype(f)
    ang = (pos[:, None] * inv[None, :]).astype(f)
    ang = np.concatenate([ang, ang], -1)
    base = (half + f(0.4 * DH)) / f(1.4 * DH)
    power = (pos - S // 2) / f(WIN // 2)
    sc = (base[None, :] ** power[:, None]).astype(f)
    sc = np.concatenate([sc, sc], -1)
    sign = np.where(np.arange(DH) < DH // 2, f(-1), f(1))[None, :]
    cos, sin = np.cos(ang).astype(f), np.sin(ang).astype(f) * sign
    tables = np.stack([cos * sc * f(8.0), sin * sc * f(8.0), cos / sc, sin / sc]).astype(f)
    tables = tables.reshape(4, T, P, DH).transpose(2, 0, 1, 3)
    i = (np.arange(P) % WIN)[:, None]
    jj = np.arange(2 * WIN)[None, :]
    bad = (jj > WIN + i) | (jj < i)
    swap = lambda m: np.concatenate([m[:, WIN:], m[:, :WIN]], 1)
    masks = [bad, swap(bad), swap(bad | (jj < WIN))]
    mask = np.stack([np.where(m, f(MASKED), f(0)) for m in masks], 1)
    under = np.zeros((GUARD + 2 - NPROD, H * S), ml_dtypes.bfloat16)
    under[GUARD - NPROD:] = 1
    w_all = np.concatenate([v["Wq"].T, v["Wk"].T, v["Wf"].T, v["Wr1"].T,
                            v["Wr2"].T.reshape(2, P, D).transpose(1, 0, 2).reshape(P, 2 * D), v["Wv"].T,
                            np.zeros((P, VC - RV), f)], 1)
    chunk = lambda a: [np.concatenate([a[o:o + n], np.zeros(P - n, f)]) for o, n in HCH]
    columns = [v[k] for k in ("bq", "bk", "g1", "b1", "g2", "b2")] + list(v["br1"].reshape(2, P))
    for l in range(LAYERS):
        columns += [v["f:ln_g"][l], v["f:ln_b"][l]] + chunk(v["f:b1"][l, :HID]) + chunk(v["f:b1"][l, HID:])
    scales = []
    for a in (v["f:q_scale"], v["f:k_scale"]):
        scales += [a, np.concatenate([a[:, DH // 2:], a[:, :DH // 2]], 1)]
    arrays = {
        "x": v["x"], "ident": np.eye(P, dtype=f), "identb": np.eye(P).astype(ml_dtypes.bfloat16),
        "later": np.ascontiguousarray(np.stack([np.eye(P, k=1), np.eye(P, k=1 - P)], 1).astype(f)),
        "mask": np.ascontiguousarray(mask.astype(ml_dtypes.bfloat16)), "tables": tables,
        "under": under, "w_all": w_all, "cols": np.stack(columns, 1), "WqvT": v["Wqv"].T,
        "rows": np.concatenate([flat(v[k]) for k in ("bf", "br2", "f:b2", "Ws", "bs")]),
        "bv": flat(v["bv"]), "bqv": flat(v["bqv"]), "scales": np.stack(scales, 1).reshape(-1),
        "wqkv": v["f:wqkv"], "wo": v["f:wo"], "w1": v["f:w1"], "w2": v["f:w2"],
    }
    arrays = {"in_" + k: np.ascontiguousarray(a) for k, a in arrays.items()}
    nc = bacc.Bacc("TRN2", target_bir_lowering=False, num_devices=1)
    tensors = {k[3:]: nc.dram_tensor(k, list(a.shape), mybir.dt.from_np(a.dtype), kind="ExternalInput").ap()
               for k, a in arrays.items()}
    out = nc.dram_tensor("out_0", list(v["x"].shape), F32, kind="ExternalOutput").ap()
    build(nc, tensors, out)
    r = run_bass_kernel_spmd(nc, [arrays], core_ids=[0])
    return r.results[0]["out_0"]
```
